# Optimizing a Trainium2 kernel written in Bass

```python
import numpy as np
import jax
import jax.numpy as jnp

def _softmax(x, axis=-1):
    return jax.nn.softmax(x, axis=axis)

def _gelu(x):
    return jax.nn.gelu(x, approximate=True)

def _silu(x):
    return jax.nn.silu(x)

def _sigmoid(x):
    return jax.nn.sigmoid(x)

def _layernorm(x, axis=-1, eps=1e-05):
    m = jnp.mean(x, axis=axis, keepdims=True)
    v = jnp.var(x, axis=axis, keepdims=True)
    return (x - m) / jnp.sqrt(v + eps)

def _scatter_add(tgt, idx, src, axis=0):
    return tgt.at[idx].add(src)

def _segment_sum(src, seg, n):
    return jax.ops.segment_sum(src, seg, n)
kernel_name = 'mk_vit_tower_cls_d1_tok_img256_r4_7d7e10'

def setup_inputs(seed: int=0):
    np.random.seed(seed)
    _w = jnp.asarray

    def _rec_inputs():
        import jax
        import jax.numpy as jnp
        _rk = jax.random.key(seed)
        x = -0.000202321 + 1.00025 * jax.random.normal(jax.random.fold_in(_rk, 1), (16, 64, 56, 56), jnp.float32)
        cls_tok = 0.02 * jax.random.normal(jax.random.fold_in(_rk, 5), (1, 1, 64), jnp.float32)
        return (x, cls_tok)
    x, cls_tok = _rec_inputs()

    def _L0_tok_setup():
        import jax, jax.numpy as jnp
        import numpy as np
        B, C, H, W = (8, 64, 56, 56)
        K = 3

        def _unfold3x3(x):
            b, c, h, w = x.shape
            xp = jnp.pad(x, ((0, 0), (0, 0), (1, 1), (1, 1)))
            patches = jnp.stack([xp[:, :, i:i + h, j:j + w] for i in range(K) for j in range(K)], axis=2)
            return patches.reshape(b, c * K * K, h * w).transpose(0, 2, 1)
        key = jax.random.key(seed)
        ks = jax.random.split(key, 8)
        d = C * K * K
        s1 = 1.0 / np.sqrt(d)
        s2 = 1.0 / np.sqrt(C)
        return {'x': jax.random.normal(ks[0], (B, C, H, W), jnp.float32), 'W1': jax.random.uniform(ks[1], (d, C), jnp.float32, -s1, s1), 'b1': jax.random.uniform(ks[2], (C,), jnp.float32, -s1, s1), 'W2': jax.random.uniform(ks[3], (C, d), jnp.float32, -s2, s2), 'b2': jax.random.uniform(ks[4], (d,), jnp.float32, -s2, s2), 'W3': jax.random.uniform(ks[5], (d, C), jnp.float32, -s1, s1), 'b3': jax.random.uniform(ks[6], (C,), jnp.float32, -s1, s1)}
    _L0_tok_all = _L0_tok_setup()
    _L0_tok_in = {k: v for k, v in _L0_tok_all.items() if k in ('W1', 'b1', 'W2', 'b2', 'W3', 'b3')}
    del _L0_tok_all

    def _L0_attn_setup():
        import jax, jax.numpy as jnp
        import numpy as np
        key = jax.random.key(seed)
        inputs = jax.random.normal(key, (8, 512, 64), dtype=jnp.float32)
        return {'inputs': inputs}
    _L0_attn_all = _L0_attn_setup()
    _L0_attn_in = {k: v for k, v in _L0_attn_all.items() if k in ()}
    del _L0_attn_all

    def _L0_ffn_setup():
        import math
        import jax, jax.numpy as jnp
        import numpy as np
        CAPACITY_FACTOR = 1.25
        key = jax.random.key(seed)
        ks = jax.random.split(key, 5)
        B, L, D, F, E = (8, 2048, 64, 256, 8)
        h = jax.random.normal(ks[0], (B, L, D), dtype=jnp.float32)
        gate_w = jax.random.normal(ks[1], (D, E), dtype=jnp.float32) * 0.02
        gate_b = jnp.zeros((E,), dtype=jnp.float32)
        w1 = jax.random.normal(ks[2], (E, D, F), dtype=jnp.float32) * (1.0 / math.sqrt(D))
        b1 = jnp.zeros((E, F), dtype=jnp.float32)
        w2 = jax.random.normal(ks[3], (E, F, D), dtype=jnp.float32) * (1.0 / math.sqrt(F))
        b2 = jnp.zeros((E, D), dtype=jnp.float32)
        return {'h': h, 'gate_w': gate_w, 'gate_b': gate_b, 'w1': w1, 'b1': b1, 'w2': w2, 'b2': b2}
    _L0_ffn_all = _L0_ffn_setup()
    _L0_ffn_in = {k: v for k, v in _L0_ffn_all.items() if k in ('gate_w', 'gate_b', 'w1', 'b1', 'w2', 'b2')}
    del _L0_ffn_all
    return {'x': x, 'cls_tok': cls_tok, 'L0_tok_W1': _L0_tok_in['W1'], 'L0_tok_b1': _L0_tok_in['b1'], 'L0_tok_W2': _L0_tok_in['W2'], 'L0_tok_b2': _L0_tok_in['b2'], 'L0_tok_W3': _L0_tok_in['W3'], 'L0_tok_b3': _L0_tok_in['b3'], 'L0_ffn_gate_w': _L0_ffn_in['gate_w'], 'L0_ffn_gate_b': _L0_ffn_in['gate_b'], 'L0_ffn_w1': _L0_ffn_in['w1'], 'L0_ffn_b1': _L0_ffn_in['b1'], 'L0_ffn_w2': _L0_ffn_in['w2'], 'L0_ffn_b2': _L0_ffn_in['b2']}

def reference(x, cls_tok, L0_tok_W1, L0_tok_b1, L0_tok_W2, L0_tok_b2, L0_tok_W3, L0_tok_b3, L0_ffn_gate_w, L0_ffn_gate_b, L0_ffn_w1, L0_ffn_b1, L0_ffn_w2, L0_ffn_b2):
    import jax
    import jax.numpy as jnp

    def _L0_tok_ref(x, W1, b1, W2, b2, W3, b3):
        import jax, jax.numpy as jnp
        import numpy as np
        B, C, H, W = (8, 64, 56, 56)
        K = 3

        def _unfold3x3(x):
            b, c, h, w = x.shape
            xp = jnp.pad(x, ((0, 0), (0, 0), (1, 1), (1, 1)))
            patches = jnp.stack([xp[:, :, i:i + h, j:j + w] for i in range(K) for j in range(K)], axis=2)
            return patches.reshape(b, c * K * K, h * w).transpose(0, 2, 1)
        t = _unfold3x3(x)
        h1 = jax.nn.relu(jnp.einsum('bld,dc->blc', t, W1) + b1)
        s = jax.nn.sigmoid(jnp.einsum('blc,cd->bld', h1, W2) + b2)
        out = jnp.einsum('bld,dc->blc', t * s, W3) + b3
        return out

    def _L0_attn_ref(inputs):
        import jax, jax.numpy as jnp
        import numpy as np
        d_k = jnp.asarray(inputs.shape[-1], dtype=inputs.dtype)
        scores = jnp.einsum('bnd,bmd->bnm', inputs, inputs) / jnp.sqrt(d_k)
        weights = jax.nn.softmax(scores, axis=-1)
        context = jnp.einsum('bnm,bmd->bnd', weights, inputs)
        return context

    def _L0_ffn_ref(h, gate_w, gate_b, w1, b1, w2, b2):
        import math
        import jax, jax.numpy as jnp
        import numpy as np
        CAPACITY_FACTOR = 1.25
        B, L, D = h.shape
        E = gate_w.shape[1]
        T = B * L
        C = max(1, math.ceil(CAPACITY_FACTOR * T / E))
        x = h.reshape(T, D)
        logits = x @ gate_w + gate_b
        probs = jax.nn.softmax(logits, axis=-1)
        idx = jnp.argmax(probs, axis=-1)
        prb = jnp.take_along_axis(probs, idx[:, None], axis=1)[:, 0]
        one_hot = jax.nn.one_hot(idx, E, dtype=jnp.float32)
        pos = (jnp.cumsum(one_hot, axis=0) * one_hot).sum(-1).astype(jnp.int32) - 1
        kept = pos < C
        pos_safe = jnp.where(kept, pos, C)
        buf = jnp.zeros((E, C, D), dtype=h.dtype).at[idx, pos_safe].set(x, mode='drop')
        hmid = jax.nn.relu(jnp.einsum('ecd,edf->ecf', buf, w1) + b1[:, None, :])
        ybuf = jnp.einsum('ecf,efd->ecd', hmid, w2) + b2[:, None, :]
        pos_g = jnp.minimum(pos, C - 1)
        y_tok = ybuf[idx, pos_g] * (prb * kept)[:, None]
        y = y_tok.reshape(B, L, D)
        y = jnp.nan_to_num(y, nan=0.0, posinf=10000.0, neginf=-10000.0)
        return y
    h = _L0_tok_ref(x, L0_tok_W1, L0_tok_b1, L0_tok_W2, L0_tok_b2, L0_tok_W3, L0_tok_b3)
    h = jnp.concatenate([jnp.broadcast_to(cls_tok, (h.shape[0], 1, h.shape[2])), h], axis=1)
    h = h + _L0_attn_ref(_layernorm(h, axis=-1))
    h = h + _L0_ffn_ref(_layernorm(h, axis=-1), L0_ffn_gate_w, L0_ffn_gate_b, L0_ffn_w1, L0_ffn_b1, L0_ffn_w2, L0_ffn_b2)
    return h

_drawn_inputs = setup_inputs


def setup_inputs(seed=0):
    import zlib

    import numpy as np

    out = dict(_drawn_inputs(seed))
    spreads = {'L0_ffn_gate_b': (0.0, 0.1), 'L0_ffn_b1': (0.0, 0.628), 'L0_ffn_b2': (0.0, 0.476)}
    factors = {'cls_tok': 17.912, 'L0_tok_b1': 5.725}
    for name, (base, spread) in spreads.items():
        noise = np.random.default_rng([zlib.crc32(name.encode()), seed]).standard_normal(out[name].shape)
        drawn = base * np.exp(spread * noise) if base else spread * noise
        out[name] = jnp.asarray(drawn.astype(out[name].dtype))
    for name, factor in factors.items():
        out[name] = (out[name] * factor).astype(out[name].dtype)
    return out
```

```python
from contextlib import ExitStack

import concourse.bass as bass
from concourse import mybir

P = 128
ALU = mybir.AluOpType
ACT = mybir.ActivationFunctionType
F32 = mybir.dt.float32
F16 = mybir.dt.float16
I32 = mybir.dt.int32
U32 = mybir.dt.uint32
AX_X = mybir.AxisListType.X
LN_EPS = 1e-5
RSQRT_MAGIC = 0x5F3759DF
PAST_END = 1 << 23
FROM = 1


def vit_block_kernel(nc, x, cls_tok, W1, b1, W2, b2, W3, b3, gate_w, gate_b, w1, fb1, w2, fb2, out):
    B, C, H, W = x.shape
    HW = H * W
    N = HW + 1
    D = C
    TAPS = 9
    E, _, FF = w1.shape
    T = B * N
    CAP = max(1, -(-5 * T // (4 * E)))
    NT = -(-N // P)
    NP = NT * P
    TAIL = N - (NT - 1) * P
    PW = W + 2
    PH = H + 2

    CROWS = 8
    NCH = H // CROWS
    CN = CROWS * W
    PAIRS = [(0, 3), (1, 4), (2, 5), (6, 7), (8, None)]
    WINDOW = [(0, 0, 0), (0, 0, 1), (0, 0, 2), (1, 2, 0), (0, 2, 2)]
    KT = len(PAIRS)
    PADS = 4

    NU = 4
    UQ = -(-N // NU)
    QA = (UQ + 1) // 2
    QB = UQ - QA
    QPAD = NU * UQ - N
    LAG = 2
    ER = 3
    STEPS = NU * NT

    GT = 4
    CS = GT * P
    NCK = 2 * -(-CAP // (2 * CS))
    CP = NCK * CS
    CHUNKS = E * NCK
    NF = FF // P
    REC = 2 * D + 4
    COL_P = 2 * D
    COL_ID = 2 * D + 1

    NG = -(-NT // 8)
    NG4 = -(-NT // 4)

    recs = nc.dram_tensor("expert_records", (E * CP + CS, REC), F32, kind="Internal").ap()
    out_rows = out.rearrange("b n d -> (b n) d")

    def group(j, size=8):
        return range(size * j, min(size * j + size, NT))

    def span(j, size=8):
        return slice(size * j, min(size * j + size, NT))

    def tiles_after(c):
        return NT if c == NCH - 1 else (1 + CN * (c + 1)) // P

    with ExitStack() as ctx:
        def sb(name, shape, dt=F32):
            return ctx.enter_context(nc.sbuf_tensor(name, shape, dt))

        def sem(name):
            return ctx.enter_context(nc.semaphore(name))

        ps = ctx.enter_context(nc.psum_tensor("ps", [P, 8 * 512], F32))

        def bank(k, n=512):
            return ps[:, 512 * k:512 * k + n]

        def pair(k):
            return ps[:, 512 * (k + 1) - QA:512 * (k + 1) + QB]

        def halves(k):
            return (ps[:, 512 * (k + 1) - QA:512 * (k + 1)], 0, QA), (ps[:, 512 * (k + 1):512 * (k + 1) + QB], QA, QB)

        w1p = sb("w1p", [P, KT, C])
        w2p = sb("w2p", [C, KT, P])
        w3p = sb("w3p", [P, KT, C])
        b1c = sb("b1c", [C, 1])
        b2f = sb("b2f", [P, TAPS])
        b2c = sb("b2c", [P, KT])
        b3r = sb("b3r", [P, C])
        clsr = sb("clsr", [1, C])
        bias_first = sb("bias_first", [P, C])
        bias_last = sb("bias_last", [P, C])
        gw = sb("gw", [D, E])
        gbr = sb("gbr", [P, E])
        fw1 = sb("fw1", [D, E, FF])
        fw2 = sb("fw2", [P, E * NF, D])
        fb1c = sb("fb1c", [P, E * NF])
        fb2r = sb("fb2r", [P, E, D])
        ident = sb("ident", [P, P])
        ident16 = sb("ident16", [P, P], F16)
        fold = sb("fold", [P, D])
        tri = sb("tri", [P, P], F16)
        ones16 = sb("ones16", [P, P], F16)
        eidx = sb("eidx", [P, NT, E])
        ebase = sb("ebase", [P, NT, E])
        segmul = sb("segmul", [P, E, NT + 1])
        valid = sb("valid", [P, NT])
        pastend = sb("pastend", [P, NT])
        idf = sb("idf", [P, NT])
        fillrec = sb("fillrec", [P, REC])
        zero = sb("zero", [P, GT * D])

        xs = sb("xs", [P, HW])
        xpa = sb("xpa", [P, PH, PW])
        xpb = sb("xpb", [P, PH, PW])
        h1 = sb("h1", [C, 2, CN])
        th = sb("th", [P, 3, CN])
        prod = sb("prod", [P, KT, NP])
        w1f = prod[:, 1, 0:TAPS * C].rearrange("p (k o) -> p k o", k=TAPS)
        w2f = prod[0:C, 2, 0:TAPS * C]
        cen = prod[:, 1, 0:NT * D].rearrange("p (t d) -> p t d", d=D)
        sqr = prod[:, 2, 0:NT * D].rearrange("p (t d) -> p t d", d=D)
        ctxT = prod[:, KT - 1, :]
        xnT = prod[0:D, 0, :]
        hbuf = sb("hbuf", [P, NT, D])
        st = sb("st", [P, 12, NT])
        v3 = sb("v3", [P, NT, 3 * D], F16)
        kA = sb("kA", [P, NP], F16)
        kB = sb("kB", [P, NP], F16)
        e32 = sb("e32", [P, ER, UQ])
        eh = sb("eh", [P, ER, UQ], F16)
        el = sb("el", [P, ER, UQ], F16)
        rs = sb("rs", [P, NT, NU])
        rec = sb("rec", [P, NT, REC])
        lg = sb("lg", [P, NT, E])
        lex = sb("lex", [P, NT, E])
        cnt = sb("cnt", [P, NT, E])
        pen = sb("pen", [P, NT, E])
        hot = sb("hot", [P, NT, E])
        hot16 = sb("hot16", [P, NT, E], F16)
        tot = sb("tot", [P, E, NT + 1])
        pre = sb("pre", [P, E, NT + 1])
        slotf = sb("slotf", [P, NT])
        slot = sb("slot", [P, NT], I32)

        flat = prod[:, :, :].rearrange("p k n -> p (k n)")
        at = [0]

        def carve(parts, n):
            at[0] += n
            assert at[0] <= KT * NP
            return flat[0:parts, at[0] - n:at[0]]

        frec = carve(P, 2 * GT * REC).rearrange("p (r g c) -> p r g c", r=2, g=GT)
        fx = carve(D, 2 * CS).rearrange("p (r n) -> p r n", r=2)
        fh = carve(P, 2 * NF * CS).rearrange("p (r f n) -> p r f n", r=2, f=NF)
        fy = carve(P, 2 * GT * D).rearrange("p (r n) -> p r n", r=2)
        fz = carve(P, 2 * GT * D).rearrange("p (r n) -> p r n", r=2)
        fo = carve(P, 2 * GT * D).rearrange("p (r n) -> p r n", r=2)
        fmask = carve(P, 2 * GT * D).rearrange("p (r n) -> p r n", r=2).bitcast(I32)
        fnan = carve(P, 2 * GT * D).rearrange("p (r n) -> p r n", r=2).bitcast(I32)

        s_w = sem("weights_loaded")
        s_cst = sem("constants_made")
        s_wp = sem("weights_packed")
        s_fill = sem("records_filled")
        s_settled = sem("settled")
        s_pool = sem("pool_chain")
        s_dve = sem("vector_chain")
        s_x = sem("image_loaded")
        s_pad = sem("image_padded")
        s_conv = sem("conv_done")
        s_h1 = sem("h1_ready")
        s_z2 = sem("tap_logits_ready")
        s_th = sem("tap_gates_ready")
        s_prod = sem("products_ready")
        s_w3 = sem("tokens_summed")
        s_hev = sem("tokens_evacuated")
        s_xn = sem("normed_ready")
        s_vh = sem("high_parts_ready")
        s_v3 = sem("low_parts_ready")
        s_ta = sem("parts_transposed")
        s_ka = sem("keys_ready")
        s_kb = sem("swapped_keys_ready")
        s_sc = sem("scores_ready")
        s_exp = sem("exp_ready")
        s_eh = sem("exp_high_ready")
        s_el = sem("exp_low_ready")
        s_pv = sem("exp_parts_used")
        s_cev = sem("context_evacuated")
        s_fold = sem("context_folded")
        s_h2 = sem("residual_ready")
        s_rec = sem("records_ready")
        s_gt = sem("router_input_transposed")
        s_gte = sem("router_input_evacuated")
        s_lg = sem("router_logits_ready")
        s_lmx = sem("router_shifted")
        s_lex = sem("router_exp_ready")
        s_hot = sem("choice_ready")
        s_cum = sem("counts_ready")
        s_slot = sem("slots_ready")
        s_base = sem("plain_rows_written")
        s_scat = sem("records_scattered")
        s_free = sem("record_buffer_free")
        f_ld = [sem("chunk_loaded_0"), sem("chunk_loaded_1")]
        f_t = sem("chunk_transposed")
        f_te = sem("chunk_evacuated")
        f_m = sem("hidden_ready")
        f_ma = sem("hidden_a_evacuated")
        f_mb = sem("hidden_b_evacuated")
        f_y = sem("expert_out_ready")
        f_ye = sem("expert_out_evacuated")
        f_o = sem("result_ready")
        f_st = [sem("result_written_0"), sem("result_written_1")]

        def settle(eng):
            eng.sem_inc(s_settled, 1)

        block = ctx.enter_context(nc.Block())
        N_LOADS = 8 + 2 * KT - 1 + 9

        @block.sync
        def _(sp):
            n = [0]
            sp.sem_inc(s_base, FROM)

            def load(dst, src):
                n[0] += 1
                sp.dma_start(dst, src).then_inc(s_w, 16)

            def load_image(b):
                for a in range(2):
                    sp.dma_start(xs[C * a:C * a + C, :],
                                 x[bass.ds(b, 1), :, :, :].rearrange("a c h w -> (a c) (h w)")).then_inc(s_x, 16)

            load_image(0)
            w1v = W1.rearrange("(c k) o -> c k o", k=TAPS)
            w3v = W3.rearrange("(c k) o -> c k o", k=TAPS)
            b2v = b2.rearrange("(c k) -> c k", k=TAPS)
            for a in range(2):
                load(w1f[C * a:C * a + C, :, :], w1v)
                load(b2f[C * a:C * a + C, :], b2v)
            load(b1c[:, :], b1.rearrange("(c a) -> c a", a=1))
            load(w2f[:, :], W2)
            load(b3r[:, :], b3.partition_broadcast(P))
            load(clsr[:, :], cls_tok.rearrange("a b d -> (a b) d"))
            for kt, (ka, kb) in enumerate(PAIRS):
                load(w3p[0:C, kt, :], w3v[:, ka, :])
                if kb is not None:
                    load(w3p[C:P, kt, :], w3v[:, kb, :])
            load(gw[:, :], gate_w)
            load(gbr[:, :], gate_b.partition_broadcast(P))
            load(fb2r[:, :, :].rearrange("p e d -> p (e d)"), fb2.rearrange("e d -> (e d)").partition_broadcast(P))
            load(fw1[:, :, :], w1.rearrange("e d f -> d e f"))
            load(fw2[:, :, :], w2.rearrange("e (f p) d -> p (e f) d", p=P))
            with nc.allow_non_contiguous_dma("4 KB of biases, one column each"):
                for e in range(4):
                    load(fb1c[:, e * 2 * NF:(e + 1) * 2 * NF],
                         fb1[2 * e:2 * e + 2, :].rearrange("e (f p) -> p (e f)", p=P))
            assert n[0] == N_LOADS, n

            def write_rows(b):
                sp.wait_ge(s_rec, b + 1)
                sp.dma_start(out[bass.ds(b, 1), 0:(NT - 1) * P, :].rearrange("a (t p) d -> p (a t) d", p=P),
                             hbuf[:, 0:NT - 1, :]).then_inc(s_base, 16)
                sp.dma_start(out[bass.ds(b, 1), (NT - 1) * P:N, :].rearrange("a p d -> (a p) d"),
                             hbuf[0:TAIL, NT - 1, :]).then_inc(s_base, 16)

            with sp.Fori(0, B - 1) as b:
                sp.wait_ge(s_pad, PADS * b + PADS)
                load_image(b + 1)
                write_rows(b)
            write_rows(B - 1)

            sp.wait_ge(s_scat, 16 * NT * B)
            sp.wait_ge(s_lg, FROM + B)
            sp.wait_ge(s_fill, 16 * (E + 1))

            def load_chunk(k, r):
                sp.dma_start(frec[:, r, :, :].rearrange("p g c -> p (g c)"),
                             recs[bass.ds(k * CS, CS), :].rearrange("(p g) c -> p (g c)", g=GT)).then_inc(f_ld[r], 16)

            load_chunk(0, 0)
            load_chunk(1, 1)
            with sp.Fori(0, CHUNKS // 2 - 1) as k:
                for r in range(2):
                    sp.wait_ge(f_st[r], (k + 1) * 16 * GT)
                    load_chunk(2 * k + 2 + r, r)
            sp.wait_ge(f_st[0], 16 * GT * (CHUNKS // 2))
            load_chunk(CHUNKS, 0)

        @block.gpsimd
        def _(pool):
            chain = [0]
            pool.sem_inc(s_free, FROM)

            def link(ins):
                chain[0] += 1
                ins.then_inc(s_pool, 1)
                pool.wait_ge(s_pool, chain[0])

            link(nc.gpsimd.memset(fillrec[:, :], 0.0))
            link(nc.gpsimd.memset(fillrec[:, COL_ID:COL_ID + 1].bitcast(I32), PAST_END))
            for k in range(E):
                pool.dma_start(recs[k * CP:(k + 1) * CP, :].rearrange("(p r) c -> p r c", p=P),
                               fillrec[:, :].unsqueeze(1).broadcast_to([P, CP // P, REC])).then_inc(s_fill, 16)
            pool.dma_start(recs[E * CP:E * CP + CS, :].rearrange("(p r) c -> p r c", p=P),
                           fillrec[:, :].unsqueeze(1).broadcast_to([P, GT, REC])).then_inc(s_fill, 16)

            for t, v in ((xpa, 0.0), (xpb, 0.0), (w2p, 0.0), (w1p, 0.0), (b2c, 0.0), (ident, 0.0), (fold, 0.0),
                         (ones16, 1.0), (tri, 1.0), (valid, 1.0), (pastend, 0.0), (segmul, 1.0), (tot, 0.0),
                         (pre, 0.0), (bias_last, 0.0), (zero, 0.0), (rec, 0.0)):
                link(nc.gpsimd.memset(t[tuple(slice(None) for _ in t.shape)], v))
            link(nc.gpsimd.memset(segmul[:, :, 0:1], 0.0))
            link(nc.gpsimd.affine_select(out=ident[:, :], in_=ident[:, :], compare_op=ALU.not_equal, fill=1.0,
                                         base=0, pattern=[[-1, P]], channel_multiplier=1))
            for a in range(2):
                link(nc.gpsimd.affine_select(out=fold[:, :], in_=fold[:, :], compare_op=ALU.not_equal, fill=1.0,
                                             base=-D * a, pattern=[[-1, D]], channel_multiplier=1))
            link(nc.gpsimd.affine_select(out=tri[:, :], in_=tri[:, :], compare_op=ALU.is_ge, fill=0.0,
                                         base=0, pattern=[[1, P]], channel_multiplier=-1))
            for t, v in ((valid, 0.0), (pastend, float(PAST_END))):
                link(nc.gpsimd.affine_select(out=t[:, NT - 1:NT], in_=t[:, NT - 1:NT], compare_op=ALU.is_ge,
                                             fill=v, base=TAIL - 1, pattern=[[0, 1]], channel_multiplier=-1))
            link(nc.gpsimd.iota(eidx[:, :, :], pattern=[[0, NT], [1, E]], base=-E, channel_multiplier=0,
                                allow_small_or_imprecise_dtypes=True))
            link(nc.gpsimd.iota(idf[:, :], pattern=[[P, NT]], base=0, channel_multiplier=1,
                                allow_small_or_imprecise_dtypes=True))
            link(nc.gpsimd.tensor_scalar(ebase[:, :, :], eidx[:, :, :], float(CP), float(E * CP - 1),
                                         ALU.mult, ALU.add))
            nc.gpsimd.tensor_copy(ident16[:, :], ident[:, :]).then_inc(s_cst, 1)
            pool.wait_ge(s_cst, 1)

            def pad_image(b):
                pool.wait_ge(s_x, 32 * b + 32)
                settle(pool)
                img = xs[:, :].rearrange("p (h w) -> p h w", h=H)
                copies = ((xpa[0:C, 1:1 + H, 1:1 + W], img[0:C]), (xpa[C:P, 0:H, 1:1 + W], img[C:P]),
                          (xpb[0:C, 1:1 + H, 1:1 + W], img[0:C]), (xpb[C:P, 1:1 + H, 0:W], img[C:P]))
                for n, (dst, src) in enumerate(copies):
                    nc.gpsimd.tensor_copy(dst, src).then_inc(s_pad, 1)
                    pool.wait_ge(s_pad, PADS * b + (n + 1))
                    settle(pool)

            def scatter_image(b):
                pool.wait_ge(s_slot, FROM + b + 1)
                settle(pool)
                for t in range(NT):
                    nc.gpsimd.indirect_dma_start(
                        recs, bass.IndirectOffsetOnAxis(slot[:, t:t + 1].bitcast(U32), 0), rec[:, t, :], None,
                        bounds_check=E * CP - 1, oob_is_err=False).then_inc(s_scat, 16)
                pool.wait_ge(s_scat, (b + 1) * (16 * NT))
                pool.sem_inc(s_free, 1)

            pad_image(0)
            pool.wait_ge(s_fill, 16 * (E + 1))
            with pool.Fori(0, B - 1) as b:
                pool.wait_ge(s_conv, (b + 1) * NCH)
                pool.wait_ge(s_prod, (b + 1) * (NCH * KT))
                pad_image(b + 1)
                scatter_image(b)
            scatter_image(B - 1)

            pool.wait_ge(s_base, FROM + 32 * B)
            with pool.Fori(0, CHUNKS // 2) as k:
                for r in range(2):
                    pool.wait_ge(f_o, 2 * k + r + 1)
                    settle(pool)
                    for g in range(GT):
                        nc.gpsimd.indirect_dma_start(
                            out_rows, bass.IndirectOffsetOnAxis(frec[:, r, g, COL_ID:COL_ID + 1].bitcast(U32), 0),
                            fo[:, r, D * g:D * g + D], None,
                            bounds_check=T - 1, oob_is_err=False).then_inc(f_st[r], 16)
            for r in range(2):
                pool.wait_ge(f_st[r], 16 * GT * (CHUNKS // 2))

        @block.tensor
        def _(pe):
            for start in (s_pv, s_lg):
                pe.sem_inc(start, FROM)

            def conv(b, c):
                if c >= 2:
                    pe.wait_ge(s_h1, b * NCH + (c - 1))
                for kt, (which, r, q) in enumerate(WINDOW):
                    src = (xpa, xpb)[which][:, r + CROWS * c:r + CROWS * (c + 1), q:q + W]
                    last = nc.tensor.matmul(bank(6 + c % 2, CN)[0:C], w1p[:, kt, :], src,
                                            start=kt == 0, stop=kt == KT - 1)
                last.then_inc(s_conv, 1)

            def tap_logits(b, c):
                pe.wait_ge(s_h1, b * NCH + (c + 1))
                for kt in range(KT):
                    n = c * KT + kt
                    if n >= 4:
                        pe.wait_ge(s_th, b * (NCH * KT) + (n - 3))
                    nc.tensor.matmul(bank(n % 4, CN), w2p[:, kt, :], h1[:, c % 2, :],
                                     start=True, stop=True).then_inc(s_z2, 1)

            def tokens(b, c):
                pe.wait_ge(s_prod, b * (NCH * KT) + KT * (c + 1))
                for t in range(tiles_after(c - 1) if c else 0, tiles_after(c)):
                    j = t // 8
                    if t % 8 == 0 and j >= 2:
                        pe.wait_ge(s_hev, b * NG + (j - 1))
                    for kt in range(KT):
                        last = nc.tensor.matmul(bank(4 + j % 2)[:, D * (t % 8):D * (t % 8 + 1)],
                                                prod[:, kt, P * t:P * t + P], w3p[:, kt, :],
                                                start=kt == 0, stop=kt == KT - 1)
                    if t % 8 == 7 or t == NT - 1:
                        last.then_inc(s_w3, 1)

            pe.wait_ge(s_cst, 1)
            pe.wait_ge(s_wp, 1)
            with pe.Fori(0, B) as b:
                pe.wait_ge(s_pad, PADS * b + PADS)
                pe.wait_ge(s_slot, FROM + b)
                conv(b, 0)
                for c in range(NCH):
                    if c + 1 < NCH:
                        conv(b, c + 1)
                    tap_logits(b, c)
                    if c:
                        tokens(b, c - 1)
                tokens(b, NCH - 1)

                pe.wait_ge(s_v3, b + 1)
                pe.wait_ge(s_vh, 2 * b + 2)
                for j in range(NG):
                    for a in range(2):
                        dst = bank(4 * a + j).bitcast(F16)
                        for i, t in enumerate(group(j)):
                            last = nc.tensor.transpose(dst[:, P * i:P * i + P], v3[:, t, D * a:D * a + 2 * D],
                                                       ident16[:, :])
                        last.then_inc(s_ta, 1)

                pe.wait_ge(s_ka, (b + 1) * NG)
                pe.wait_ge(s_kb, (b + 1) * NG)
                settle(pe)
                with pe.Fori(0, NU) as u:
                    for m in range(NT + LAG):
                        if m < NT:
                            if m >= 2:
                                pe.wait_ge(s_exp, b * STEPS + u * NT + (m - 1))
                            for dst, off, n in halves(2 * (m % 2)):
                                for keys in (kA, kB):
                                    last = nc.tensor.matmul(dst, kA[:, P * m:P * m + P],
                                                            keys[:, bass.ds(u * UQ + off, n)],
                                                            start=keys is kA, stop=keys is kB)
                            last.then_inc(s_sc, 1)
                        if m >= LAG:
                            k = m - LAG
                            if k == 0:
                                pe.wait_ge(s_cev, FROM + b * NU + u)
                            pe.wait_ge(s_el, FROM + b * STEPS + u * NT + (k + 1))
                            for part in (eh, el):
                                for dst, off, n in halves(4):
                                    last = nc.tensor.matmul(dst, v3[:, k, 0:2 * D], part[:, k % ER, off:off + n],
                                                            start=k == 0 and part is eh,
                                                            stop=k == NT - 1 and part is el)
                            last.then_inc(s_pv, 1)

                pe.wait_ge(s_cev, FROM + (b + 1) * NU)
                for j in range(NG):
                    for i, t in enumerate(group(j)):
                        last = nc.tensor.matmul(bank((6, 7, 0, 1)[j])[:, D * i:D * i + D], ctxT[:, P * t:P * t + P],
                                                fold[:, :], start=True, stop=True)
                    last.then_inc(s_fold, 1)

                pe.wait_ge(s_rec, b + 1)
                settle(pe)
                for j in range(NG4):
                    if j >= 4:
                        pe.wait_ge(s_gte, b * NG4 + (j - 3))
                        settle(pe)
                    for i, t in enumerate(group(j, 4)):
                        last = nc.tensor.transpose(bank(2 + j % 4)[0:D, P * i:P * i + P], rec[:, t, 0:D], ident[:, :])
                    last.then_inc(s_gt, 1)
                pe.wait_ge(s_gte, (b + 1) * NG4)
                for t in range(NT):
                    last = nc.tensor.matmul(bank(6)[:, E * t:E * t + E], xnT[:, P * t:P * t + P], gw[:, :],
                                            start=True, stop=True)
                last.then_inc(s_lg, 1)

                pe.wait_ge(s_hot, b + 1)
                hv = hot16[:, :, :].rearrange("p t e -> p (t e)")
                nc.tensor.matmul(bank(7, NT * E), tri[:, :], hv, start=True, stop=True)
                nc.tensor.matmul(bank(0, NT * E), ones16[:, :], hv, start=True, stop=True).then_inc(s_cum, 1)

            pe.wait_ge(s_slot, FROM + B)

            def chunk_transpose(k, r, nth):
                pe.wait_ge(f_ld[r], 16 * nth)
                settle(pe)
                for g in range(GT):
                    last = nc.tensor.transpose(bank(r)[0:D, P * g:P * g + P], frec[:, r, g, 0:D], ident[:, :])
                last.then_inc(f_t, 1)

            chunk_transpose(0, 0, 1)
            for e in range(E):
                with pe.Fori(0, NCK // 2) as kk:
                    for r in range(2):
                        k = kk * 2 + (e * NCK + r)
                        pe.wait_ge(f_te, k + 1)
                        for f in range(NF):
                            last = nc.tensor.matmul(bank(2 + 2 * r + f), fw1[:, e, P * f:P * f + P], fx[:, r, :],
                                                    start=True, stop=True)
                        last.then_inc(f_m, 1)
                        chunk_transpose(k + 1, 1 - r, kk + (e * NCK // 2 + 1 + r))
                        pe.wait_ge(f_ma, k + 1)
                        pe.wait_ge(f_mb, k + 1)
                        pe.wait_ge(f_ye, FROM + k)
                        for g in range(GT):
                            for f in range(NF):
                                last = nc.tensor.matmul(bank(6 + r)[:, D * g:D * g + D],
                                                        fh[:, r, f, P * g:P * g + P], fw2[:, e * NF + f, :],
                                                        start=f == 0, stop=f == NF - 1)
                        last.then_inc(f_y, 1)

        @block.scalar
        def _(act):
            def relu(b, c):
                act.wait_ge(s_conv, b * NCH + (c + 1))
                if c >= 2:
                    act.wait_ge(s_z2, b * (NCH * KT) + KT * (c - 1))
                nc.scalar.activation(h1[:, c % 2, :], bank(6 + c % 2, CN)[0:C], ACT.Relu,
                                     bias=b1c[:, :]).then_inc(s_h1, 1)

            act.sem_inc(s_cev, FROM)
            act.wait_ge(s_wp, 1)
            act.wait_ge(s_cst, 1)
            with act.Fori(0, B) as b:
                relu(b, 0)
                for c in range(NCH):
                    if c + 1 < NCH:
                        relu(b, c + 1)
                    for kt in range(KT):
                        n = c * KT + kt
                        act.wait_ge(s_z2, b * (NCH * KT) + (n + 1))
                        if n >= 3:
                            act.wait_ge(s_prod, b * (NCH * KT) + (n - 2))
                        nc.scalar.activation(th[:, n % 3, :], bank(n % 4, CN), ACT.Tanh, scale=0.5,
                                             bias=b2c[:, kt:kt + 1]).then_inc(s_th, 1)

                act.wait_ge(s_xn, b + 1)
                nc.scalar.copy(v3[:, :, 0:D], sqr[:, :, :]).then_inc(s_vh, 1)
                nc.scalar.copy(v3[:, :, 2 * D:3 * D], sqr[:, :, :]).then_inc(s_vh, 1)
                for j in range(NG):
                    act.wait_ge(s_ta, b * (2 * NG) + (2 * j + 1))
                    n = len(group(j)) * P
                    nc.scalar.copy(kA[:, 8 * P * j:8 * P * j + n], bank(j).bitcast(F16)[:, 0:n]).then_inc(s_ka, 1)

                with act.Fori(0, NU) as u:
                    for m in range(NT):
                        act.wait_ge(s_sc, b * STEPS + u * NT + (m + 1))
                        act.wait_ge(s_el, FROM + b * STEPS + u * NT + max(m - ER + 1, 0))
                        nc.scalar.activation(e32[:, m % ER, :], pair(2 * (m % 2)), ACT.Exp, scale=float(D) ** -0.5,
                                             accum_out=rs[:, m, bass.ds(u, 1)]).then_inc(s_exp, 1)
                    act.wait_ge(s_pv, FROM + b * STEPS + (u + 1) * NT)
                    nc.scalar.copy(ctxT[:, bass.ds(u * UQ, UQ)], pair(4)).then_inc(s_cev, 1)

                for j in range(NG4):
                    act.wait_ge(s_gt, b * NG4 + (j + 1))
                    n = len(group(j, 4)) * P
                    nc.scalar.copy(xnT[:, 4 * P * j:4 * P * j + n], bank(2 + j % 4, n)[0:D]).then_inc(s_gte, 1)
                act.wait_ge(s_lmx, b + 1)
                nc.scalar.activation(lex[:, :, :], lg[:, :, :], ACT.Exp).then_inc(s_lex, 1)

            def evacuate_input(k, r):
                act.wait_ge(f_t, k + 1)
                nc.scalar.copy(fx[:, r, :], bank(r)[0:D]).then_inc(f_te, 1)

            evacuate_input(0, 0)
            for e in range(E):
                with act.Fori(0, NCK // 2) as kk:
                    for r in range(2):
                        k = kk * 2 + (e * NCK + r)
                        act.wait_ge(f_m, k + 1)
                        nc.scalar.activation(fh[:, r, 0, :], bank(2 + 2 * r), ACT.Relu,
                                             bias=fb1c[:, e * NF:e * NF + 1]).then_inc(f_ma, 1)
                        evacuate_input(k + 1, 1 - r)

        @block.vector
        def _(dve):
            seen = [0]
            base = [0]

            def link(ins, apart=False):
                seen[0] += 1
                ins.then_inc(s_dve, 1)
                dve.wait_ge(s_dve, base[0] + seen[0])
                if apart:
                    settle(dve)

            def over(v, n):
                return v.unsqueeze(2).broadcast_to([P, NT, n])

            for start_ in (s_slot, s_el, f_ye):
                dve.sem_inc(start_, FROM)

            dve.wait_ge(s_w, 16 * N_LOADS)
            dve.wait_ge(s_cst, 1)
            w2v = w2f[:, :].rearrange("p (c k) -> p k c", k=TAPS)
            link(nc.vector.memset(w3p[C:P, KT - 1, :], 0.0))
            for kt, (ka, kb) in enumerate(PAIRS):
                link(nc.vector.tensor_copy(w1p[0:C, kt, :], w1f[0:C, ka, :]))
                link(nc.vector.tensor_copy(w2p[:, kt, 0:C], w2v[:, ka, :]))
                link(nc.vector.tensor_scalar(b2c[0:C, kt:kt + 1], b2f[0:C, ka:ka + 1], 0.5, None, ALU.mult))
                if kb is not None:
                    link(nc.vector.tensor_copy(w1p[C:P, kt, :], w1f[C:P, kb, :]))
                    link(nc.vector.tensor_copy(w2p[:, kt, C:P], w2v[:, kb, :]))
                    link(nc.vector.tensor_scalar(b2c[C:P, kt:kt + 1], b2f[C:P, kb:kb + 1], 0.5, None, ALU.mult))
            link(nc.vector.tensor_scalar(w3p[:, :, :], w3p[:, :, :], 0.5, None, ALU.mult))
            link(nc.vector.tensor_copy(bias_first[:, :], b3r[:, :]))
            link(nc.vector.tensor_copy(bias_first[0:1, :], clsr[:, :]))
            link(nc.vector.memset(hbuf[:, :, :], 0.0))
            nc.vector.tensor_copy(bias_last[0:TAIL, :], b3r[0:TAIL, :]).then_inc(s_wp, 1)

            def layernorm(src, dst):
                mean, var, half, y = st[:, 0, :], st[:, 1, :], st[:, 2, :], st[:, 3, :]
                t, y2 = st[:, 4, :], st[:, 5, :]
                link(nc.vector.tensor_reduce(mean, src, AX_X, ALU.add))
                link(nc.vector.tensor_scalar(mean, mean, 1.0 / D, None, ALU.mult))
                link(nc.vector.tensor_tensor(cen[:, :, :], src, over(mean, D), ALU.subtract))
                link(nc.vector.tensor_tensor(sqr[:, :, :], cen[:, :, :], cen[:, :, :], ALU.mult))
                link(nc.vector.tensor_reduce(var, sqr[:, :, :], AX_X, ALU.add))
                link(nc.vector.tensor_scalar(var, var, 1.0 / D, LN_EPS, ALU.mult, ALU.add))
                link(nc.vector.tensor_scalar(half.bitcast(I32), var.bitcast(I32), 1, None,
                                             ALU.logical_shift_right))
                link(nc.vector.tensor_scalar(y.bitcast(I32), half.bitcast(I32), -1.0, float(RSQRT_MAGIC),
                                             ALU.mult, ALU.add))
                for _ in range(4):
                    link(nc.vector.scalar_tensor_tensor(out=t, in0=y, scalar=-0.5, in1=y,
                                                        op0=ALU.mult, op1=ALU.mult))
                    link(nc.vector.tensor_tensor(t, t, var, ALU.mult))
                    link(nc.vector.scalar_tensor_tensor(out=y2, in0=t, scalar=1.5, in1=y,
                                                        op0=ALU.add, op1=ALU.mult))
                    y, y2 = y2, y
                return nc.vector.tensor_tensor(dst, cen[:, :, :], over(y, D), ALU.mult)

            PER_IMAGE = 72
            start = seen[0]
            with dve.Fori(0, B) as b:
                seen[0] = 0
                base[0] = b * PER_IMAGE + start

                dve.wait_ge(s_lg, FROM + b)
                link(nc.vector.memset(prod[:, :, 0:1], 0.0))
                link(nc.vector.memset(prod[:, :, N:NP], 0.0))
                dve.wait_ge(s_base, FROM + 32 * b)

                def add_bias(j):
                    dve.wait_ge(s_w3, b * NG + (j + 1))
                    src = bank(4 + j % 2).rearrange("p (t d) -> p t d", d=D)
                    t0, t1 = group(j)[0], group(j)[-1] + 1
                    cuts = sorted({t0, t1} | ({1} if t0 == 0 else set()) | ({NT - 1} if t1 == NT else set()))
                    for a, z in zip(cuts, cuts[1:]):
                        bias = bias_first if a == 0 else bias_last if a == NT - 1 else b3r
                        last = nc.vector.tensor_tensor(hbuf[:, a:z, :], src[:, a - t0:z - t0, :],
                                                       bias[:, :].unsqueeze(1).broadcast_to([P, z - a, D]), ALU.add)
                    last.then_inc(s_hev, 1)

                for c in range(NCH):
                    for kt, (which, r, q) in enumerate(WINDOW):
                        n = c * KT + kt
                        dve.wait_ge(s_th, b * (NCH * KT) + (n + 1))
                        nc.vector.scalar_tensor_tensor(
                            out=prod[:, kt, 1 + CN * c:1 + CN * (c + 1)].rearrange("p (h w) -> p h w", w=W),
                            in0=th[:, n % 3, :].rearrange("p (h w) -> p h w", w=W), scalar=1.0,
                            in1=(xpa, xpb)[which][:, r + CROWS * c:r + CROWS * (c + 1), q:q + W],
                            op0=ALU.add, op1=ALU.mult).then_inc(s_prod, 1)
                    for j in range(NG):
                        done = tiles_after(c - 1) if c else 0
                        before = tiles_after(c - 2) if c >= 2 else 0
                        if before < group(j)[-1] + 1 <= done:
                            add_bias(j)
                for j in range(NG):
                    if tiles_after(NCH - 2) < group(j)[-1] + 1:
                        add_bias(j)
                dve.wait_ge(s_hev, (b + 1) * NG)

                layernorm(hbuf[:, :, :], sqr[:, :, :]).then_inc(s_xn, 1)
                dve.wait_ge(s_vh, 2 * b + 1)
                dve.wait_ge(s_xn, b + 1)
                nc.vector.tensor_tensor(v3[:, :, D:2 * D], sqr[:, :, :], v3[:, :, 0:D],
                                        ALU.subtract).then_inc(s_v3, 1)
                for j in range(NG):
                    dve.wait_ge(s_ta, b * (2 * NG) + (2 * j + 2))
                    n = len(group(j)) * P
                    nc.vector.tensor_copy(kB[:, 8 * P * j:8 * P * j + n],
                                          bank(4 + j).bitcast(F16)[:, 0:n]).then_inc(s_kb, 1)

                with dve.Fori(0, NU) as u:
                    for m in range(NT + 1):
                        if m < NT:
                            dve.wait_ge(s_exp, b * STEPS + u * NT + (m + 1))
                            dve.wait_ge(s_pv, FROM + b * STEPS + u * NT + max(m - ER + 1, 0))
                            nc.vector.tensor_copy(eh[:, m % ER, :], e32[:, m % ER, :]).then_inc(s_eh, 1)
                        if m >= 1:
                            k = m - 1
                            dve.wait_ge(s_eh, b * STEPS + u * NT + (k + 1))
                            nc.vector.tensor_tensor(el[:, k % ER, :], e32[:, k % ER, :], eh[:, k % ER, :],
                                                    ALU.subtract).then_inc(s_el, 1)

                total, inv = st[:, 6, :], st[:, 7, :]
                link(nc.vector.tensor_reduce(total, rs[:, :, :], AX_X, ALU.add))
                link(nc.vector.tensor_scalar(total, total, float(-QPAD), None, ALU.add))
                link(nc.vector.reciprocal(inv, total))
                for j in range(NG):
                    dve.wait_ge(s_fold, b * NG + (j + 1))
                    s = span(j)
                    k = len(group(j))
                    link(nc.vector.tensor_tensor(
                        cen[:, s, :], bank((6, 7, 0, 1)[j], D * k).rearrange("p (t d) -> p t d", d=D),
                        inv[:, s].unsqueeze(2).broadcast_to([P, k, D]), ALU.mult))
                link(nc.vector.tensor_tensor(hbuf[:, :, :], hbuf[:, :, :], cen[:, :, :], ALU.add))

                dve.wait_ge(s_free, FROM + b)
                link(nc.vector.tensor_copy(rec[:, :, D:2 * D], hbuf[:, :, :]))
                layernorm(hbuf[:, :, :], rec[:, :, 0:D]).then_inc(s_rec, 1)

                mx, best, esum = st[:, 8, :], st[:, 9, :], st[:, 10, :]
                dve.wait_ge(s_lg, FROM + b + 1)
                link(nc.vector.tensor_tensor(lg[:, :, :], bank(6, NT * E).rearrange("p (t e) -> p t e", e=E),
                                             gbr[:, :].unsqueeze(1).broadcast_to([P, NT, E]), ALU.add))
                link(nc.vector.tensor_reduce(mx, lg[:, :, :], AX_X, ALU.max))
                nc.vector.tensor_tensor(lg[:, :, :], lg[:, :, :], over(mx, E), ALU.subtract).then_inc(s_lmx, 1)
                dve.wait_ge(s_lmx, b + 1)
                link(nc.vector.tensor_scalar(hot[:, :, :], lg[:, :, :], 0.0, float(-E), ALU.is_equal, ALU.mult))
                link(nc.vector.scalar_tensor_tensor(out=hot[:, :, :], in0=eidx[:, :, :], scalar=float(E),
                                                    in1=hot[:, :, :], op0=ALU.add, op1=ALU.add))
                link(nc.vector.tensor_reduce(best, hot[:, :, :], AX_X, ALU.min))
                link(nc.vector.tensor_tensor(hot[:, :, :], eidx[:, :, :], over(best, E), ALU.is_equal))
                link(nc.vector.tensor_tensor(hot[:, :, :], hot[:, :, :], over(valid[:, :], E), ALU.mult))
                nc.vector.tensor_copy(hot16[:, :, :], hot[:, :, :]).then_inc(s_hot, 1)
                dve.wait_ge(s_lex, b + 1)
                link(nc.vector.tensor_reduce(esum, lex[:, :, :], AX_X, ALU.add))
                link(nc.vector.reciprocal(rec[:, :, COL_P], esum))
                link(nc.vector.tensor_copy(rec[:, :, COL_ID].bitcast(I32), idf[:, :]))
                link(nc.vector.tensor_scalar(idf[:, :], idf[:, :], float(N), None, ALU.add))

                link(nc.vector.tensor_copy(tot[:, :, 0], pre[:, :, NT]))
                dve.wait_ge(s_cum, b + 1)
                link(nc.vector.tensor_copy(tot[:, :, 1:NT + 1],
                                           bank(0, NT * E).rearrange("p (t e) -> p e t", e=E)))
                link(nc.vector.tensor_tensor_scan(pre[:, :, :].rearrange("p e t -> p (e t)"),
                                                  segmul[:, :, :].rearrange("p e t -> p (e t)"),
                                                  tot[:, :, :].rearrange("p e t -> p (e t)"), 0.0,
                                                  ALU.mult, ALU.add))
                link(nc.vector.tensor_tensor(cnt[:, :, :], bank(7, NT * E).rearrange("p (t e) -> p t e", e=E),
                                             pre[:, :, 0:NT].rearrange("p e t -> p t e"), ALU.add))
                link(nc.vector.tensor_scalar(pen[:, :, :], cnt[:, :, :], float(CAP), float(PAST_END),
                                             ALU.is_gt, ALU.mult))
                link(nc.vector.tensor_tensor(cnt[:, :, :], cnt[:, :, :], ebase[:, :, :], ALU.add))
                link(nc.vector.tensor_tensor(cnt[:, :, :], cnt[:, :, :], pen[:, :, :], ALU.add))
                link(nc.vector.tensor_tensor(cnt[:, :, :], cnt[:, :, :], hot[:, :, :], ALU.mult))
                link(nc.vector.tensor_reduce(slotf[:, :], cnt[:, :, :], AX_X, ALU.add))
                link(nc.vector.tensor_tensor(slotf[:, :], slotf[:, :], pastend[:, :], ALU.add))
                nc.vector.tensor_copy(slot[:, :], slotf[:, :]).then_inc(s_slot, 1)
                assert seen[0] == PER_IMAGE, seen[0]

            start += B * PER_IMAGE
            PER_CHUNK = 4
            for e in range(E):
                with dve.Fori(0, NCK // 2) as kk:
                    for r in range(2):
                        k = kk * 2 + (e * NCK + r)
                        seen[0] = 0
                        base[0] = k * PER_CHUNK + start
                        dve.wait_ge(f_m, k + 1)
                        nc.vector.tensor_scalar(fh[:, r, 1, :], bank(3 + 2 * r), fb1c[:, e * NF + 1:e * NF + 2], 0.0,
                                                ALU.add, ALU.max).then_inc(f_mb, 1)
                        dve.wait_ge(f_y, k + 1)
                        y3 = fy[:, r, :].rearrange("p (g d) -> p g d", d=D)
                        z3 = fz[:, r, :].rearrange("p (g d) -> p g d", d=D)
                        nc.vector.tensor_tensor(y3, bank(6 + r, GT * D).rearrange("p (g d) -> p g d", d=D),
                                                fb2r[:, e, :].unsqueeze(1).broadcast_to([P, GT, D]),
                                                ALU.add).then_inc(f_ye, 1)
                        dve.wait_ge(f_ye, FROM + k + 1)
                        link(nc.vector.tensor_tensor(z3, y3, frec[:, r, :, COL_P:COL_P + 1].broadcast_to([P, GT, D]),
                                                     ALU.mult))
                        nc.vector.tensor_scalar(fmask[:, r, :], fz[:, r, :], 0.0, 0.0, ALU.mult, ALU.is_equal)
                        nc.vector.tensor_tensor(fnan[:, r, :], fz[:, r, :], fz[:, r, :], ALU.not_equal)
                        link(nc.vector.tensor_scalar(fy[:, r, :], fz[:, r, :], -1e4, 1e4, ALU.max, ALU.min),
                             apart=True)
                        link(nc.vector.copy_predicated(fy[:, r, :], fmask[:, r, :], fz[:, r, :]), apart=True)
                        link(nc.vector.copy_predicated(fy[:, r, :], fnan[:, r, :], zero[:, :]))
                        nc.vector.tensor_tensor(fo[:, r, :].rearrange("p (g d) -> p g d", d=D), y3,
                                                frec[:, r, :, D:2 * D], ALU.add).then_inc(f_o, 1)
                        assert seen[0] == PER_CHUNK, seen[0]


_INS = ['x', 'cls_tok', 'L0_tok_W1', 'L0_tok_b1', 'L0_tok_W2', 'L0_tok_b2', 'L0_tok_W3', 'L0_tok_b3',
        'L0_ffn_gate_w', 'L0_ffn_gate_b', 'L0_ffn_w1', 'L0_ffn_b1', 'L0_ffn_w2', 'L0_ffn_b2']


def kernel(**inputs):
    import numpy as _np
    import concourse.bacc as _bacc
    from concourse import mybir as _mybir
    from concourse.bass_utils import run_bass_kernel_spmd as _run

    nc = _bacc.Bacc("TRN2", target_bir_lowering=False, num_devices=1)
    arrays, args = {}, []
    for name in _INS:
        a = _np.ascontiguousarray(inputs[name])
        arrays[f"in_{name}_dram"] = a
        args.append(nc.dram_tensor(f"in_{name}_dram", a.shape, _mybir.dt.from_np(a.dtype), kind="ExternalInput").ap())
    B, C, H, W = inputs["x"].shape
    args.append(nc.dram_tensor("out_0_dram", (B, H * W + 1, C), _mybir.dt.float32, kind="ExternalOutput").ap())
    vit_block_kernel(nc, *args)
    r = _run(nc, [arrays], core_ids=[0])
    return r.results[0]["out_0_dram"]
```

```python
from contextlib import ExitStack

import concourse.bass as bass
from concourse import mybir

P = 128
ALU = mybir.AluOpType
ACT = mybir.ActivationFunctionType
F32 = mybir.dt.float32
F16 = mybir.dt.float16
BF16 = mybir.dt.bfloat16
I32 = mybir.dt.int32
U32 = mybir.dt.uint32
AX_X = mybir.AxisListType.X
LN_EPS = 1e-5
RSQRT_MAGIC = 0x5F3759DF
PAST_END = 1 << 23
FROM = 1
FROM2 = 2


class Chain:

    def __init__(self, eng, sem, settled, per=0):
        self.eng, self.sem, self.settled, self.per = eng, sem, settled, per
        self.base, self.n = 0, 0

    def at(self, round_, n=0):
        self.base, self.n = round_ * self.per, n

    def link(self, ins, apart=False):
        self.n += 1
        ins.then_inc(self.sem, 1)
        self.eng.wait_ge(self.sem, self.base + self.n)
        if apart:
            self.eng.sem_inc(self.settled, 1)

    def ends(self):
        assert self.n == self.per, (self.n, self.per)


def vit_block_kernel(nc, x, cls_tok, W1, b1, W2, b2, W3, b3, gate_w, gate_b, w1, fb1, w2, fb2, out):
    B, C, H, W = x.shape
    HW = H * W
    N = HW + 1
    D = C
    TAPS = 9
    E, _, FF = w1.shape
    T = B * N
    CAP = max(1, -(-5 * T // (4 * E)))
    NT = -(-N // P)
    NP = NT * P
    TAIL = N - (NT - 1) * P
    PW = W + 2
    PH = H + 2

    CROWS = 8
    NCH = H // CROWS
    CN = CROWS * W
    PAIRS = [(0, 3), (1, 4), (2, 5), (6, 7), (8, None)]
    WINDOW = [(0, 0, 0), (0, 0, 1), (0, 0, 2), (1, 2, 0), (0, 2, 2)]
    KT = len(PAIRS)
    SUPER = 2 * CN // P
    SW = 1 + 2 * CN
    HALVES = 2
    HROWS = H // HALVES
    PADS = 4 * HALVES

    NU = 4
    UQ = -(-N // NU)
    QA = (UQ + 1) // 2
    QB = UQ - QA
    QPAD = NU * UQ - N
    LAG = 3
    ER = 3
    HR = 4
    ROUND = 2 * NT
    STEPS = NU * NT

    def twice(g):
        return g % 5 in (1, 3)

    def casts(g):
        return sum(not twice(k) for k in range(g))

    CASTS = casts(ROUND)

    FT = (N + E * (P - 1)) // P
    GT = 8
    assert FT % (2 * GT) == 0
    NF = FF // P
    WP = 3
    REC = 2 * D + 4
    COL_P = 2 * D
    COL_ID = 2 * D + 1

    NG = -(-NT // 8)
    NG4 = -(-NT // 4)
    SPLIT = 16

    recs = nc.dram_tensor("expert_records", (FT * P, REC), F32, kind="Internal").ap()
    out_rows = out.rearrange("b n d -> (b n) d")

    def group(j, size=8):
        return range(size * j, min(size * j + size, NT))

    def span(j, size=8):
        return slice(size * j, min(size * j + size, NT))

    def tiles_after(c):
        return NT if c == NCH - 1 else (1 + CN * (c + 1)) // P

    with ExitStack() as ctx:
        def sb(name, shape, dt=F32):
            return ctx.enter_context(nc.sbuf_tensor(name, shape, dt))

        def sem(name):
            return ctx.enter_context(nc.semaphore(name))

        ps = ctx.enter_context(nc.psum_tensor("ps", [P, 8 * 512], F32))

        def bank(k, n=512):
            return ps[:, 512 * k:512 * k + n]

        def pair(k):
            return ps[:, 512 * (k + 1) - QA:512 * (k + 1) + QB]

        def halves(k):
            return (ps[:, 512 * (k + 1) - QA:512 * (k + 1)], 0, QA), (ps[:, 512 * (k + 1):512 * (k + 1) + QB], QA, QB)

        Z2B = 3
        TOKEN_BANK = (4, 5)
        CONV_BANK = 6
        FOLD_BANK = (3, 7, 4, 5)
        ROUTER_BANK = (3, 7)
        LOGIT_BANK = 3
        COUNT_BANK = 7
        TURN_BANK = ((0, 1), (2, 6), (0, 1), (2, 6))
        FX_BANK, FH_BANK, FY_BANK = (4, 5), ((0, 1), (2, 3)), (6, 7)

        w1p = sb("w1p", [P, KT, C])
        w2p = sb("w2p", [C, KT, P])
        w3p = sb("w3p", [P, KT, C])
        b1c = sb("b1c", [C, 1])
        b2c = sb("b2c", [P, KT])
        b3r = sb("b3r", [P, C])
        bias_first = sb("bias_first", [P, C])
        bias_last = sb("bias_last", [P, C])
        gw = sb("gw", [D, E])
        gbr = sb("gbr", [P, E])
        fw1 = sb("fw1", [P, WP, E * FF], BF16)
        fw2 = sb("fw2", [P, E * NF * D])
        fb1c = sb("fb1c", [P, E, NF])
        fb2r = sb("fb2r", [1, E * D])
        ident = sb("ident", [P, P])
        ident16 = sb("ident16", [P, P], F16)
        fold = sb("fold", [P, D])
        tri = sb("tri", [P, P], F16)
        ones16 = sb("ones16", [P, P], F16)
        ones1 = sb("ones1", [1, P])
        eidx = sb("eidx", [P, FT, E])
        tileno = sb("tileno", [P, FT, E])
        segmul = sb("segmul", [P, E, NT + 1])
        valid = sb("valid", [P, NT])
        pastend = sb("pastend", [P, NT])
        idf = sb("idf", [P, NT])
        oldest = sb("oldest", [P, 1])
        fillrec = sb("fillrec", [P, REC])
        zero = sb("zero", [P, GT * D])

        xs = sb("xs", [P, HROWS * W])
        xpa = sb("xpa", [P, PH, PW])
        xpb = sb("xpb", [P, PH, PW])
        h1 = sb("h1", [C, 2, CN])
        th = sb("th", [P, 3, CN])
        prod = sb("prod", [P, 2, KT, SW])
        hbuf = sb("hbuf", [P, NT, D])
        st = sb("st", [P, 12, NT])
        v3 = sb("v3", [P, NT, 3 * D], F16)
        kA = sb("kA", [P, NP], F16)
        kB = sb("kB", [P, NP], F16)
        ctxT = sb("ctxT", [P, NP])
        rs = sb("rs", [P, NT, NU])
        rec = sb("rec", [P, NT, REC])
        rec16 = rec[:, :, 0:D].bitcast(F16)
        lg = sb("lg", [P, NT, E])
        lex = sb("lex", [P, NT, E])
        cnt = sb("cnt", [P, NT, E])
        pen = sb("pen", [P, NT, E])
        hot = sb("hot", [P, NT, E])
        hot16 = sb("hot16", [P, NT, E], F16)
        tot = sb("tot", [P, E, NT + 1])
        pre = sb("pre", [P, E, NT + 1])
        seen = sb("seen", [P, E])
        em = sb("em", [P, 8, E])
        emi = sb("emi", [P, E], I32)
        slotf = sb("slotf", [P, NT])
        slot = sb("slot", [P, NT], I32)
        ehot = sb("ehot", [P, FT, E])
        eprod = sb("eprod", [P, FT, E])
        ejf = sb("ejf", [P, FT])
        ej = sb("ej", [P, FT], I32)
        fbias = sb("fbias", [P, NF, FT])

        HALF = (HR * UQ + 1) // 2
        att = sb("att", [P, ER * UQ + 2 * HALF])
        e32 = att[:, 0:ER * UQ].rearrange("p (r n) -> p r n", r=ER)
        eh = att[:, ER * UQ:ER * UQ + HALF].bitcast(F16)[:, 0:HR * UQ].rearrange("p (r n) -> p r n", r=HR)
        el = att[:, ER * UQ + HALF:ER * UQ + 2 * HALF].bitcast(F16)[:, 0:HR * UQ].rearrange("p (r n) -> p r n", r=HR)
        cen = att[:, 0:NT * D].rearrange("p (t d) -> p t d", d=D)
        sqr = att[:, NT * D:2 * NT * D].rearrange("p (t d) -> p t d", d=D)
        xnT = att[0:D, 2 * NT * D:2 * NT * D + 2 * 4 * P].rearrange("p (r n) -> p r n", r=2)
        assert 2 * NT * D + 2 * 4 * P <= ER * UQ + 2 * HALF

        frec = sb("frec", [P, 2, GT, REC])
        frec16 = frec[:, :, :, 0:D].bitcast(F16)
        fo = sb("fo", [P, 2, GT * D])
        fstale = sb("fstale", [P, 2, GT])
        fidx = sb("fidx", [P, 2, GT], I32)

        flat = prod[:, :, :, :].rearrange("p a k n -> p (a k n)")
        fx = flat[:, 0:GT * P].bitcast(F16).rearrange("p (r n) -> p r n", r=2)
        fh = flat[:, 1024:1024 + 4 * NF * P].rearrange("p (r f n) -> p r f n", r=2, f=NF)
        fz = flat[:, 2048:2048 + 2 * GT * D].rearrange("p (r n) -> p r n", r=2)
        fmask = flat[:, 3072:3072 + GT * D].bitcast(I32)
        fnan = flat[:, 3584:3584 + GT * D].bitcast(I32)

        w1f = flat[:, 0:TAPS * C].rearrange("p (k o) -> p k o", k=TAPS)
        w2f = flat[0:C, 600:600 + TAPS * C]
        b2f = flat[:, 1200:1200 + TAPS]
        clsr = flat[0:1, 1220:1220 + C]
        fw1f = flat[:, 1300:1300 + E * FF]
        fw1r = flat[:, 3400:3400 + E * FF]
        assert 3400 + E * FF <= 2 * KT * SW

        s_w = sem("weights_loaded")
        s_cst = sem("constants_made")
        s_wp = sem("weights_packed")
        s_fill = sem("records_filled")
        s_settled = sem("settled")
        s_pool = sem("pool_chain")
        s_old = sem("oldest_row_moved")
        s_dw = sem("vector_weights_chain")
        s_dt = sem("vector_token_chain")
        s_dp = sem("vector_post_chain")
        s_df = sem("vector_expert_chain")
        s_x = sem("image_loaded")
        s_pad = sem("image_padded")
        s_conv = sem("conv_done")
        s_h1 = sem("h1_ready")
        s_z2 = sem("tap_logits_ready")
        s_th = sem("tap_gates_ready")
        s_prod = sem("products_ready")
        s_tk = sem("products_used")
        s_w3 = sem("tokens_summed")
        s_hev = sem("tokens_evacuated")
        s_xn = sem("normed_ready")
        s_vh = sem("high_parts_ready")
        s_v3 = sem("low_parts_ready")
        s_ta = sem("parts_transposed")
        s_ka = sem("keys_ready")
        s_sc = sem("scores_ready")
        s_exp = sem("exp_ready")
        s_eh = sem("exp_high_ready")
        s_el = sem("exp_low_ready")
        s_pv = sem("exp_parts_used")
        s_cev = sem("context_evacuated")
        s_fold = sem("context_folded")
        s_fev = sem("folded_evacuated")
        s_h2 = sem("residual_ready")
        s_cen = sem("centered_ready")
        s_sq = sem("squares_ready")
        s_xn2 = sem("second_normed_ready")
        s_rh = sem("record_high_ready")
        s_rl = sem("record_low_ready")
        s_gt = sem("router_input_transposed")
        s_gte = sem("router_input_evacuated")
        s_gl = sem("router_input_used")
        s_lg = sem("router_logits_ready")
        s_lmx = sem("router_shifted")
        s_lex = sem("router_exp_ready")
        s_hot = sem("choice_ready")
        s_cum = sem("counts_ready")
        s_slot = sem("slots_ready")
        s_ej = sem("tile_experts_ready")
        s_base = sem("plain_rows_written")
        s_scat = sem("records_scattered")
        s_free = sem("record_buffer_free")
        f_ld = [sem("group_loaded_0"), sem("group_loaded_1")]
        f_t = sem("group_transposed")
        f_te = sem("group_evacuated")
        f_m = sem("hidden_ready")
        f_ma = sem("hidden_a_evacuated")
        f_mb = sem("hidden_b_evacuated")
        f_y = sem("expert_out_ready")
        f_ye = sem("expert_out_evacuated")
        f_o = sem("result_ready")
        f_st = [sem("result_written_0"), sem("result_written_1")]
        f_free = sem("result_buffer_free")

        def settle(eng):
            eng.sem_inc(s_settled, 1)

        block = ctx.enter_context(nc.Block())
        N_LOADS = 8 + 2 * KT - 1 + 2 + 6

        @block.sync
        def _(sp):
            n = [0]
            sp.sem_inc(s_base, FROM)

            def load(dst, src):
                n[0] += 1
                sp.dma_start(dst, src).then_inc(s_w, 16)

            w1v = W1.rearrange("(c k) o -> c k o", k=TAPS)
            w3v = W3.rearrange("(c k) o -> c k o", k=TAPS)
            b2v = b2.rearrange("(c k) -> c k", k=TAPS)
            for a in range(2):
                load(w1f[C * a:C * a + C, :, :], w1v)
                load(b2f[C * a:C * a + C, :], b2v)
            load(b1c[:, :], b1.rearrange("(c a) -> c a", a=1))
            load(w2f, W2)
            load(b3r[:, :], b3.partition_broadcast(P))
            load(clsr, cls_tok.rearrange("a b d -> (a b) d"))
            for kt, (ka, kb) in enumerate(PAIRS):
                load(w3p[0:C, kt, :], w3v[:, ka, :])
                if kb is not None:
                    load(w3p[C:P, kt, :], w3v[:, kb, :])
            load(gw[:, :], gate_w)
            load(gbr[:, :], gate_b.partition_broadcast(P))
            load(fb2r[:, :], fb2.rearrange("(a e) d -> a (e d)", a=1))
            for a in range(2):
                load(fw1f[D * a:D * a + D, :].rearrange("p (e f) -> p e f", e=E), w1.rearrange("e d f -> d e f"))
            load(fw2[:, :].rearrange("p (e d) -> p e d", d=D), w2.rearrange("e (f p) d -> p (e f) d", p=P))
            with nc.allow_non_contiguous_dma("8 KB of biases, one column each"):
                for f in range(NF):
                    load(fb1c[:, :, f], fb1[:, P * f:P * f + P].rearrange("e p -> p e"))
            assert n[0] == N_LOADS, n

            def write_rows(b):
                sp.wait_ge(s_h2, b + 1)
                sp.dma_start(out[bass.ds(b, 1), 0:(NT - 1) * P, :].rearrange("a (t p) d -> p (a t) d", p=P),
                             rec[:, 0:NT - 1, D:2 * D]).then_inc(s_base, 16)
                sp.dma_start(out[bass.ds(b, 1), (NT - 1) * P:N, :].rearrange("a p d -> (a p) d"),
                             rec[0:TAIL, NT - 1, D:2 * D]).then_inc(s_base, 16)

            def load_groups(i):
                for rnd in range(2):
                    for r in range(2):
                        sp.wait_ge(f_o, i * 4 + (2 * rnd + r + 1))
                        g = 2 * rnd + r
                        sp.dma_start(frec[:, r, :, :],
                                     recs[P * GT * g:P * GT * (g + 1), :].rearrange("(g p) c -> p g c", p=P)
                                     ).then_inc(f_ld[r], 16)

            sp.wait_ge(s_fill, 16)
            load_groups(0)
            write_rows(0)
            with sp.Fori(1, B) as b:
                sp.wait_ge(s_scat, b * (16 * NT))
                load_groups(b)
                write_rows(b)
            sp.wait_ge(s_scat, B * (16 * NT))
            load_groups(B)

        @block.gpsimd
        def _(pool):
            chain = Chain(pool, s_pool, s_settled)
            link = chain.link
            pool.sem_inc(s_free, FROM)
            pool.sem_inc(f_free, FROM2)

            link(nc.gpsimd.memset(fillrec[:, :], 0.0))
            link(nc.gpsimd.memset(fillrec[:, COL_ID:COL_ID + 1], float(PAST_END)))
            pool.dma_start(recs.rearrange("(p r) c -> p r c", p=P),
                           fillrec[:, :].unsqueeze(1).broadcast_to([P, FT, REC])).then_inc(s_fill, 16)

            for t, v in ((xpa, 0.0), (xpb, 0.0), (w2p, 0.0), (w1p, 0.0), (b2c, 0.0), (ident, 0.0), (fold, 0.0),
                         (ones16, 1.0), (ones1, 1.0), (tri, 1.0), (valid, 1.0), (pastend, 0.0), (segmul, 1.0),
                         (tot, 0.0), (seen, 0.0), (bias_last, 0.0), (zero, 0.0), (rec, 0.0), (ctxT, 0.0),
                         (ej, 0), (fbias, 0.0), (oldest, float(-N)), (em, 0.0)):
                link(nc.gpsimd.memset(t[tuple(slice(None) for _ in t.shape)], v))
            link(nc.gpsimd.memset(segmul[:, :, 0:1], 0.0))
            link(nc.gpsimd.affine_select(out=ident[:, :], in_=ident[:, :], compare_op=ALU.not_equal, fill=1.0,
                                         base=0, pattern=[[-1, P]], channel_multiplier=1))
            for a in range(2):
                link(nc.gpsimd.affine_select(out=fold[:, :], in_=fold[:, :], compare_op=ALU.not_equal, fill=1.0,
                                             base=-D * a, pattern=[[-1, D]], channel_multiplier=1))
            link(nc.gpsimd.affine_select(out=tri[:, :], in_=tri[:, :], compare_op=ALU.is_ge, fill=0.0,
                                         base=0, pattern=[[1, P]], channel_multiplier=-1))
            for t, v in ((valid, 0.0), (pastend, float(PAST_END))):
                link(nc.gpsimd.affine_select(out=t[:, NT - 1:NT], in_=t[:, NT - 1:NT], compare_op=ALU.is_ge,
                                             fill=v, base=TAIL - 1, pattern=[[0, 1]], channel_multiplier=-1))
            link(nc.gpsimd.iota(eidx[:, :, :], pattern=[[0, FT], [1, E]], base=0, channel_multiplier=0,
                                allow_small_or_imprecise_dtypes=True))
            link(nc.gpsimd.iota(tileno[:, :, :], pattern=[[1, FT], [0, E]], base=0, channel_multiplier=0,
                                allow_small_or_imprecise_dtypes=True))
            link(nc.gpsimd.iota(idf[:, :], pattern=[[P, NT]], base=0, channel_multiplier=1,
                                allow_small_or_imprecise_dtypes=True))
            nc.gpsimd.tensor_copy(ident16[:, :], ident[:, :]).then_inc(s_cst, 1)
            pool.wait_ge(s_cst, 1)

            def pad_image(b):
                for hf in range(HALVES):
                    r0 = hf * HROWS
                    for a in range(2):
                        pool.dma_start(xs[C * a:C * a + C, :],
                                       x[bass.ds(b, 1), :, r0:r0 + HROWS, :].rearrange("a c h w -> (a c) (h w)")
                                       ).then_inc(s_x, 16)
                    pool.wait_ge(s_x, (b * HALVES + (hf + 1)) * 32)
                    settle(pool)
                    img = xs[:, :].rearrange("p (h w) -> p h w", w=W)
                    copies = ((xpa[0:C, 1 + r0:1 + r0 + HROWS, 1:1 + W], img[0:C]),
                              (xpa[C:P, r0:r0 + HROWS, 1:1 + W], img[C:P]),
                              (xpb[0:C, 1 + r0:1 + r0 + HROWS, 1:1 + W], img[0:C]),
                              (xpb[C:P, 1 + r0:1 + r0 + HROWS, 0:W], img[C:P]))
                    for n, (dst, src) in enumerate(copies):
                        nc.gpsimd.tensor_copy(dst, src).then_inc(s_pad, 1)
                        pool.wait_ge(s_pad, b * PADS + (4 * hf + n + 1))
                        settle(pool)

            def record_low(b):
                pool.wait_ge(s_rh, b + 1)
                settle(pool)
                nc.gpsimd.tensor_tensor(rec16[:, :, D:2 * D], sqr, rec16[:, :, 0:D], ALU.subtract).then_inc(s_rl, 1)
                pool.wait_ge(s_rl, b + 1)
                settle(pool)

            def scatter_image(b):
                for r in range(2):
                    pool.wait_ge(f_ld[r], (b + 1) * 32)
                pool.wait_ge(s_slot, FROM + b + 1)
                settle(pool)
                for t in range(NT):
                    nc.gpsimd.indirect_dma_start(
                        recs, bass.IndirectOffsetOnAxis(slot[:, t:t + 1].bitcast(U32), 0), rec[:, t, :], None,
                        bounds_check=FT * P - 1, oob_is_err=False).then_inc(s_scat, 16)
                pool.wait_ge(s_scat, (b + 1) * (16 * NT))
                pool.sem_inc(s_free, 1)

            def scatter_results(i):
                pool.wait_ge(s_base, FROM + i * 32)
                for g in range(4):
                    r = g % 2
                    pool.wait_ge(f_o, FROM2 + i * 4 + (g + 1))
                    settle(pool)
                    for t in range(GT):
                        nc.gpsimd.indirect_dma_start(
                            out_rows, bass.IndirectOffsetOnAxis(fidx[:, r, t:t + 1].bitcast(U32), 0),
                            fo[:, r, D * t:D * t + D], None,
                            bounds_check=T - 1, oob_is_err=False).then_inc(f_st[r], 16)
                    pool.wait_ge(f_st[r], i * (32 * GT) + 16 * GT * (g // 2 + 1))
                    pool.sem_inc(f_free, 1)

            pad_image(0)
            with pool.Fori(0, B - 1) as b:
                pool.wait_ge(s_conv, (b + 1) * NCH)
                pool.wait_ge(s_prod, (b + 1) * (NCH * KT))
                settle(pool)
                pad_image(b + 1)
                scatter_results(b)
                record_low(b)
                scatter_image(b)
            scatter_results(B - 1)
            record_low(B - 1)
            scatter_image(B - 1)
            scatter_results(B)

        @block.tensor
        def _(pe):
            for start in (s_pv, s_lg):
                pe.sem_inc(start, FROM)

            def conv(t, c):
                if c >= 1:
                    pe.wait_ge(s_h1, t * NCH + c)
                for kt, (which, r, q) in enumerate(WINDOW):
                    src = (xpa, xpb)[which][:, r + CROWS * c:r + CROWS * (c + 1), q:q + W]
                    last = nc.tensor.matmul(bank(CONV_BANK, CN)[0:C], w1p[:, kt, :], src,
                                            start=kt == 0, stop=kt == KT - 1)
                last.then_inc(s_conv, 1)

            def tap_logits(t, c):
                pe.wait_ge(s_h1, t * NCH + (c + 1))
                for kt in range(KT):
                    n = c * KT + kt
                    if n >= Z2B:
                        pe.wait_ge(s_th, t * (NCH * KT) + (n - Z2B + 1))
                    nc.tensor.matmul(bank(n % Z2B, CN), w2p[:, kt, :], h1[:, c % 2, :],
                                     start=True, stop=True).then_inc(s_z2, 1)

            def tokens(t, c):
                pe.wait_ge(s_prod, t * (NCH * KT) + KT * (c + 1))
                for k in range(tiles_after(c - 1) if c else 0, tiles_after(c)):
                    j = k // 8
                    if k % 8 == 0 and j >= 2:
                        pe.wait_ge(s_hev, t * NG + (j - 1))
                    s, i = divmod(k, SUPER)
                    for kt in range(KT):
                        last = nc.tensor.matmul(bank(TOKEN_BANK[j % 2])[:, D * (k % 8):D * (k % 8 + 1)],
                                                prod[:, s % 2, kt, P * i:P * i + P], w3p[:, kt, :],
                                                start=kt == 0, stop=kt == KT - 1)
                    if k % 8 == 7 or k == NT - 1:
                        last.then_inc(s_w3, 1)
                if c < NCH - 1:
                    last.then_inc(s_tk, 1)

            def turn(t, j):
                part = 0 if 8 * (j + 1) <= SPLIT else 1
                pe.wait_ge(s_v3, t * 2 + part + 1)
                if j >= 2:
                    pe.wait_ge(s_ka, t * (2 * NG) + 2 * (j - 1))
                for a in range(2):
                    dst = bank(TURN_BANK[j][a]).bitcast(F16)
                    for i, k in enumerate(group(j)):
                        last = nc.tensor.transpose(dst[:, P * i:P * i + P], v3[:, k, D * a:D * a + 2 * D],
                                                   ident16[:, :])
                    last.then_inc(s_ta, 1)

            def attention_round(b, p):
                base = b * STEPS + p * ROUND
                for g in range(ROUND + LAG):
                    if g < ROUND:
                        u, m = divmod(g, NT)
                        if g >= 2:
                            pe.wait_ge(s_exp, base + (g - 1))
                        for dst, off, n in halves(2 * (g % 2)):
                            for keys in (kA, kB):
                                last = nc.tensor.matmul(dst, kA[:, P * m:P * m + P],
                                                        keys[:, bass.ds(p * (2 * UQ) + (u * UQ + off), n)],
                                                        start=keys is kA, stop=keys is kB)
                        last.then_inc(s_sc, 1)
                    if g >= LAG:
                        k = g - LAG
                        u, m = divmod(k, NT)
                        if m == 0:
                            pe.wait_ge(s_cev, FROM + b * NU + p * 2)
                            pe.wait_ge(s_slot, FROM + b)
                        pe.wait_ge(s_el, FROM + base + (k + 1))
                        for part in (eh, el):
                            for dst, off, n in halves(4 + 2 * u):
                                last = nc.tensor.matmul(dst, v3[:, m, 0:2 * D], part[:, k % HR, off:off + n],
                                                        start=m == 0 and part is eh, stop=m == NT - 1 and part is el)
                        last.then_inc(s_pv, 1)

            def expert_round(i, p, attended=True):
                pe.wait_ge(s_ej, FROM + i)
                settle(pe)
                if attended:
                    pe.wait_ge(s_cev, FROM + i * NU + (p * 2 + 2))
                    settle(pe)
                for r in range(2):
                    pe.wait_ge(f_ld[r], i * 32 + (p * 16 + 16))
                    settle(pe)
                    dst = bank(FX_BANK[r]).bitcast(F16)
                    for t in range(GT):
                        last = nc.tensor.transpose(dst[:, P * t:P * t + P], frec16[:, r, t, :], ident16[:, :])
                    last.then_inc(f_t, 1)
                for r in range(2):
                    experts = nc.values_load_multi_w_load_instructions(
                        ej[0:1, bass.ds(p * (2 * GT) + r * GT, GT)], engines=[pe.engine], min_val=0, max_val=E - 1,
                        skip_runtime_bounds_check_because="clamped on the chip to 0..E-1")[1]
                    pe.wait_ge(f_te, i * 4 + p * 2 + (r + 1))
                    first = i * (FT // 2) + p * GT + r * (GT // 2)

                    def hidden(q):
                        if r or q >= 2:
                            pe.wait_ge(f_ma, first + (q - 1))
                            pe.wait_ge(f_mb, first + (q - 1))
                        for f in range(NF):
                            for t in (2 * q, 2 * q + 1):
                                for w in range(WP):
                                    last = nc.tensor.matmul(bank(FH_BANK[q % 2][f])[:, P * (t % 2):P * (t % 2) + P],
                                                            fw1[:, w, bass.ds(experts[t] * FF + P * f, P)],
                                                            fx[:, r, P * t:P * t + P], start=w == 0,
                                                            stop=w == WP - 1)
                        last.then_inc(f_m, 1)

                    def result(q):
                        pe.wait_ge(f_ma, first + (q + 1))
                        pe.wait_ge(f_mb, first + (q + 1))
                        for t in (2 * q, 2 * q + 1):
                            dst = bank(FY_BANK[r])[:, D * t:D * t + D]
                            for f in range(NF):
                                nc.tensor.matmul(dst, fh[:, q % 2, f, P * (t % 2):P * (t % 2) + P],
                                                 fw2[:, bass.ds(experts[t] * (NF * D) + D * f, D)],
                                                 start=f == 0, stop=False)
                            last = nc.tensor.matmul(dst, ones1[:, :], fb2r[:, bass.ds(experts[t] * D, D)],
                                                    start=False, stop=True)
                        return last

                    hidden(0)
                    for q in range(GT // 2):
                        if q + 1 < GT // 2:
                            hidden(q + 1)
                        last = result(q)
                    last.then_inc(f_y, 1)

            def fold_context(b):
                pe.wait_ge(s_cev, FROM + (b + 1) * NU)
                pe.wait_ge(f_ye, b * 4 + 4)
                for j in range(NG):
                    for i, k in enumerate(group(j)):
                        last = nc.tensor.matmul(bank(FOLD_BANK[j])[:, D * i:D * i + D], ctxT[:, P * k:P * k + P],
                                                fold[:, :], start=True, stop=True)
                    last.then_inc(s_fold, 1)

            def turn_router(b, j):
                if j < NG4:
                    if j == 0:
                        pe.wait_ge(s_xn2, b + 1)
                        pe.wait_ge(s_fev, (b + 1) * NG)
                    else:
                        pe.wait_ge(s_gte, b * NG4 + j)
                    settle(pe)
                    for i, k in enumerate(group(j, 4)):
                        last = nc.tensor.transpose(bank(ROUTER_BANK[1])[0:D, P * i:P * i + P], sqr[:, k, :],
                                                   ident[:, :])
                    last.then_inc(s_gt, 1)

            def router_logits(b, j):
                pe.wait_ge(s_gte, b * NG4 + (j + 1))
                for i, k in enumerate(group(j, 4)):
                    last = nc.tensor.matmul(bank(LOGIT_BANK)[:, E * k:E * k + E], xnT[:, j % 2, P * i:P * i + P],
                                            gw[:, :], start=True, stop=True)
                last.then_inc(s_gl if j < NG4 - 1 else s_lg, 1)

            def router_step(b, j):
                turn_router(b, j)
                if j >= 1:
                    router_logits(b, j - 1)

            def count(b):
                pe.wait_ge(s_hot, b + 1)
                hv = hot16[:, :, :].rearrange("p t e -> p (t e)")
                nc.tensor.matmul(bank(COUNT_BANK)[:, 0:NT * E], tri[:, :], hv, start=True, stop=True)
                nc.tensor.matmul(bank(COUNT_BANK)[:, 256:256 + NT * E], ones16[:, :], hv,
                                 start=True, stop=True).then_inc(s_cum, 1)

            def mix(b, post, tok):
                t = b + 1
                if post:
                    fold_context(b)
                if tok:
                    pe.wait_ge(s_pad, t * PADS + PADS)
                    conv(t, 0)
                steps = {2: (0, 1, 2), 3: (3, 4, 5), 4: (6, 7, None)}
                for c in range(NCH):
                    todo = steps.get(c, (None, None, None)) if post else (None, None, None)
                    if tok and c + 1 < NCH:
                        conv(t, c + 1)
                    if todo[0] is not None:
                        router_step(b, todo[0])
                    if tok:
                        tap_logits(t, c)
                    if todo[1] is not None:
                        router_step(b, todo[1])
                    if post and c == 5:
                        count(b)
                    if tok and c:
                        if post and c == 1:
                            pe.wait_ge(s_fev, (b + 1) * NG)
                        tokens(t, c - 1)
                    if todo[2] is not None:
                        router_step(b, todo[2])
                if tok:
                    tokens(t, NCH - 1)
                    for j in range(NG):
                        turn(t, j)

            pe.wait_ge(s_cst, 1)
            pe.wait_ge(s_wp, 1)
            mix(-1, False, True)

            def attend(b):
                pe.wait_ge(s_ka, (b + 1) * (2 * NG))
                settle(pe)
                with pe.Fori(0, 2) as p:
                    attention_round(b, p)
                    expert_round(b, p)

            with pe.Fori(0, B - 1) as b:
                attend(b)
                mix(b, True, True)
            attend(B - 1)
            mix(B - 1, True, False)
            with pe.Fori(0, 2) as p:
                expert_round(B, p, attended=False)

        @block.scalar
        def _(act):
            act.sem_inc(s_cev, FROM)

            def relu(t, c):
                act.wait_ge(s_conv, t * NCH + (c + 1))
                if c >= 2:
                    act.wait_ge(s_z2, t * (NCH * KT) + KT * (c - 1))
                nc.scalar.activation(h1[:, c % 2, :], bank(CONV_BANK, CN)[0:C], ACT.Relu,
                                     bias=b1c[:, :]).then_inc(s_h1, 1)

            def tap_gates(t, c):
                for kt in range(KT):
                    n = c * KT + kt
                    act.wait_ge(s_z2, t * (NCH * KT) + (n + 1))
                    if n >= 3:
                        act.wait_ge(s_prod, t * (NCH * KT) + (n - 2))
                    nc.scalar.activation(th[:, n % 3, :], bank(n % Z2B, CN), ACT.Tanh, scale=0.5,
                                         bias=b2c[:, kt:kt + 1]).then_inc(s_th, 1)

            def high_parts(t, part):
                act.wait_ge(s_xn, t * 2 + (part + 1))
                s = slice(0, SPLIT) if part == 0 else slice(SPLIT, NT)
                n = s.stop - s.start
                nc.scalar.copy(v3[:, s, :].rearrange("p t (a d) -> p t a d", d=D)[:, :, 0:3:2, :],
                               sqr[:, s, :].unsqueeze(2).broadcast_to([P, n, 2, D])).then_inc(s_vh, 1)

            def keys_out(t, j):
                for a, dst in enumerate((kA, kB)):
                    act.wait_ge(s_ta, t * (2 * NG) + (2 * j + a + 1))
                    n = len(group(j)) * P
                    nc.scalar.copy(dst[:, 8 * P * j:8 * P * j + n],
                                   bank(TURN_BANK[j][a]).bitcast(F16)[:, 0:n]).then_inc(s_ka, 1)

            def router_evacuate(b, j):
                act.wait_ge(s_gt, b * NG4 + (j + 1))
                if j >= 2:
                    act.wait_ge(s_gl, b * (NG4 - 1) + (j - 1))
                n = len(group(j, 4)) * P
                nc.scalar.copy(xnT[:, j % 2, 0:n], bank(ROUTER_BANK[1], n)[0:D]).then_inc(s_gte, 1)

            def mix(b, post, tok):
                t = b + 1
                steps = {2: (0, 1, 2), 3: (3, 4, 5), 4: (6,)}
                if tok:
                    relu(t, 0)
                for c in range(NCH):
                    todo = steps.get(c, ()) if post else ()
                    if tok and c + 1 < NCH:
                        relu(t, c + 1)
                    if len(todo) > 0:
                        router_evacuate(b, todo[0])
                    if tok:
                        tap_gates(t, c)
                    for j in todo[1:]:
                        router_evacuate(b, j)
                    if post and c == 0:
                        act.wait_ge(s_cen, b + 1)
                        nc.scalar.activation(sqr, cen, ACT.Square).then_inc(s_sq, 1)
                    if post and c == 1:
                        act.wait_ge(s_xn2, b + 1)
                        nc.scalar.copy(rec16[:, :, 0:D], sqr).then_inc(s_rh, 1)
                    if post and c == 5:
                        act.wait_ge(s_lmx, b + 1)
                        nc.scalar.activation(lex[:, :, :], lg[:, :, :], ACT.Exp).then_inc(s_lex, 1)
                if tok:
                    high_parts(t, 0)
                    keys_out(t, 0)
                    keys_out(t, 1)
                    high_parts(t, 1)
                    keys_out(t, 2)
                    keys_out(t, 3)

            def attention_round(b, p):
                base = b * STEPS + p * ROUND

                def context_out(u):
                    act.wait_ge(s_pv, FROM + base + (u + 1) * NT)
                    nc.scalar.copy(ctxT[:, bass.ds(p * (2 * UQ) + u * UQ, UQ)], pair(4 + 2 * u)).then_inc(s_cev, 1)

                for g in range(ROUND):
                    u, m = divmod(g, NT)
                    act.wait_ge(s_sc, base + (g + 1))
                    if twice(g):
                        act.wait_ge(s_pv, FROM + base + max(g - HR + 1, 0))
                        nc.scalar.activation(eh[:, g % HR, :], pair(2 * (g % 2)), ACT.Exp, scale=float(D) ** -0.5)
                    act.wait_ge(s_el, FROM + base + max(g - ER + 1, 0))
                    nc.scalar.activation(e32[:, g % ER, :], pair(2 * (g % 2)), ACT.Exp, scale=float(D) ** -0.5,
                                         accum_out=rs[:, m, bass.ds(p * 2 + u, 1)]).then_inc(s_exp, 1)
                    if g == NT + LAG + 1:
                        context_out(0)
                context_out(1)

            def expert_round(i, p):
                for r in range(2):
                    act.wait_ge(f_t, i * 4 + p * 2 + (r + 1))
                    nc.scalar.copy(fx[:, r, :], bank(FX_BANK[r]).bitcast(F16)).then_inc(f_te, 1)
                for r in range(2):
                    for t in range(GT):
                        q = t // 2
                        act.wait_ge(f_m, i * (FT // 2) + p * GT + (r * (GT // 2) + q + 1))
                        ins = nc.scalar.activation(fh[:, q % 2, 0, P * (t % 2):P * (t % 2) + P],
                                                   bank(FH_BANK[q % 2][0])[:, P * (t % 2):P * (t % 2) + P], ACT.Relu,
                                                   bias=fbias[:, 0, bass.ds(p * (2 * GT) + r * GT + t, 1)])
                        if t % 2:
                            ins.then_inc(f_ma, 1)
                    act.wait_ge(f_y, i * 4 + p * 2 + (r + 1))
                    nc.scalar.copy(fz[:, r, :], bank(FY_BANK[r])).then_inc(f_ye, 1)

            act.wait_ge(s_wp, 1)
            act.wait_ge(s_cst, 1)
            mix(-1, False, True)

            def attend(b):
                with act.Fori(0, 2) as p:
                    attention_round(b, p)
                    expert_round(b, p)

            with act.Fori(0, B - 1) as b:
                attend(b)
                mix(b, True, True)
            attend(B - 1)
            mix(B - 1, True, False)
            with act.Fori(0, 2) as p:
                expert_round(B, p)

        @block.vector
        def _(dve):
            weights = Chain(dve, s_dw, s_settled)
            tokc = Chain(dve, s_dt, s_settled, 45)
            postc = Chain(dve, s_dp, s_settled, 60)
            expc = Chain(dve, s_df, s_settled, 16)

            def over(v, n, k=None):
                return v.unsqueeze(2).broadcast_to([P, k or v.shape[1], n])

            for start, v in ((s_slot, FROM), (s_el, FROM), (s_ej, FROM), (f_o, FROM2)):
                dve.sem_inc(start, v)

            link = weights.link
            dve.wait_ge(s_w, 16 * N_LOADS)
            dve.wait_ge(s_cst, 1)
            w2v = w2f.rearrange("p (c k) -> p k c", k=TAPS)
            link(nc.vector.memset(w3p[C:P, KT - 1, :], 0.0))
            for kt, (ka, kb) in enumerate(PAIRS):
                link(nc.vector.tensor_copy(w1p[0:C, kt, :], w1f[0:C, ka, :]))
                link(nc.vector.tensor_copy(w2p[:, kt, 0:C], w2v[:, ka, :]))
                link(nc.vector.tensor_scalar(b2c[0:C, kt:kt + 1], b2f[0:C, ka:ka + 1], 0.5, None, ALU.mult))
                if kb is not None:
                    link(nc.vector.tensor_copy(w1p[C:P, kt, :], w1f[C:P, kb, :]))
                    link(nc.vector.tensor_copy(w2p[:, kt, C:P], w2v[:, kb, :]))
                    link(nc.vector.tensor_scalar(b2c[C:P, kt:kt + 1], b2f[C:P, kb:kb + 1], 0.5, None, ALU.mult))
            link(nc.vector.tensor_scalar(w3p[:, :, :], w3p[:, :, :], 0.5, None, ALU.mult))
            link(nc.vector.tensor_copy(bias_first[:, :], b3r[:, :]))
            link(nc.vector.tensor_copy(bias_first[0:1, :], clsr))
            link(nc.vector.memset(hbuf[:, :, :], 0.0))
            link(nc.vector.tensor_copy(bias_last[0:TAIL, :], b3r[0:TAIL, :]))
            src = fw1f
            for w in range(WP):
                link(nc.vector.tensor_copy(fw1[:, w, :], src))
                if w + 1 < WP:
                    link(nc.vector.tensor_tensor(fw1r, src, fw1[:, w, :], ALU.subtract))
                    src = fw1r
            nc.vector.tensor_copy(st[:, 0, 0:1], b3r[:, 0:1]).then_inc(s_wp, 1)
            dve.wait_ge(s_wp, 1)

            def center(link, src, s):
                mean = st[:, 0, s]
                link(nc.vector.tensor_reduce(mean, src[:, s, :], AX_X, ALU.add))
                link(nc.vector.tensor_scalar(mean, mean, 1.0 / D, None, ALU.mult))
                return nc.vector.tensor_tensor(cen[:, s, :], src[:, s, :], over(mean, D), ALU.subtract)

            def normalize(link, s):
                var, half, y, y2, t = st[:, 1, s], st[:, 2, s], st[:, 3, s], st[:, 5, s], st[:, 4, s]
                link(nc.vector.tensor_reduce(var, sqr[:, s, :], AX_X, ALU.add))
                link(nc.vector.tensor_scalar(var, var, 1.0 / D, LN_EPS, ALU.mult, ALU.add))
                link(nc.vector.tensor_scalar(half.bitcast(I32), var.bitcast(I32), 1, None,
                                             ALU.logical_shift_right))
                link(nc.vector.tensor_scalar(y.bitcast(I32), half.bitcast(I32), -1.0, float(RSQRT_MAGIC),
                                             ALU.mult, ALU.add))
                for _ in range(4):
                    link(nc.vector.scalar_tensor_tensor(out=t, in0=y, scalar=-0.5, in1=y,
                                                        op0=ALU.mult, op1=ALU.mult))
                    link(nc.vector.tensor_tensor(t, t, var, ALU.mult))
                    link(nc.vector.scalar_tensor_tensor(out=y2, in0=t, scalar=1.5, in1=y,
                                                        op0=ALU.add, op1=ALU.mult))
                    y, y2 = y2, y
                return nc.vector.tensor_tensor(sqr[:, s, :], cen[:, s, :], over(y, D), ALU.mult)

            def products(t, c):
                s, hf = divmod(c, 2)
                if hf == 0:
                    if s >= 2:
                        dve.wait_ge(s_tk, t * (NCH - 1) + (c - 2))
                    if s == 0:
                        tokc.link(nc.vector.memset(prod[:, 0, :, 0:1], 0.0))
                    else:
                        tokc.link(nc.vector.tensor_copy(prod[:, s % 2, :, 0:1], prod[:, 1 - s % 2, :, 2 * CN:SW]))
                    if c == NCH - 1:
                        tokc.link(nc.vector.memset(prod[:, s % 2, :, 1 + CN:(NT - SUPER * s) * P], 0.0))
                for kt, (which, r, q) in enumerate(WINDOW):
                    n = c * KT + kt
                    dve.wait_ge(s_th, t * (NCH * KT) + (n + 1))
                    nc.vector.scalar_tensor_tensor(
                        out=prod[:, s % 2, kt, 1 + CN * hf:1 + CN * (hf + 1)].rearrange("p (h w) -> p h w", w=W),
                        in0=th[:, n % 3, :].rearrange("p (h w) -> p h w", w=W), scalar=1.0,
                        in1=(xpa, xpb)[which][:, r + CROWS * c:r + CROWS * (c + 1), q:q + W],
                        op0=ALU.add, op1=ALU.mult).then_inc(s_prod, 1)
                if hf == 1:
                    dve.wait_ge(s_prod, t * (NCH * KT) + KT * (c + 1))

            def add_bias(t, j):
                dve.wait_ge(s_w3, t * NG + (j + 1))
                src = bank(TOKEN_BANK[j % 2]).rearrange("p (t d) -> p t d", d=D)
                t0, t1 = group(j)[0], group(j)[-1] + 1
                cuts = sorted({t0, t1} | ({1} if t0 == 0 else set()) | ({NT - 1} if t1 == NT else set()))
                for a, z in zip(cuts, cuts[1:]):
                    bias = bias_first if a == 0 else bias_last if a == NT - 1 else b3r
                    last = nc.vector.tensor_tensor(hbuf[:, a:z, :], src[:, a - t0:z - t0, :],
                                                   bias[:, :].unsqueeze(1).broadcast_to([P, z - a, D]), ALU.add)
                last.then_inc(s_hev, 1)
                dve.wait_ge(s_hev, t * NG + (j + 1))

            def first_norm(t, part):
                s = slice(0, SPLIT) if part == 0 else slice(SPLIT, NT)
                tokc.link(center(tokc.link, hbuf, s))
                tokc.link(nc.vector.tensor_tensor(sqr[:, s, :], cen[:, s, :], cen[:, s, :], ALU.mult))
                normalize(tokc.link, s).then_inc(s_xn, 1)

            def low_parts(t, part):
                s = slice(0, SPLIT) if part == 0 else slice(SPLIT, NT)
                dve.wait_ge(s_vh, t * 2 + (part + 1))
                dve.wait_ge(s_xn, t * 2 + (part + 1))
                nc.vector.tensor_tensor(v3[:, s, D:2 * D], sqr[:, s, :], v3[:, s, 0:D],
                                        ALU.subtract).then_inc(s_v3, 1)

            def residual(b):
                link = postc.link
                total, inv = st[:, 6, :], st[:, 7, :]
                link(nc.vector.tensor_reduce(total, rs[:, :, :], AX_X, ALU.add))
                link(nc.vector.tensor_scalar(total, total, float(-QPAD), None, ALU.add))
                link(nc.vector.reciprocal(inv, total))
                for j in range(NG):
                    dve.wait_ge(s_fold, b * NG + (j + 1))
                    s, k = span(j), len(group(j))
                    nc.vector.tensor_tensor(
                        cen[:, s, :], bank(FOLD_BANK[j], D * k).rearrange("p (t d) -> p t d", d=D),
                        over(inv[:, s], D), ALU.mult).then_inc(s_fev, 1)
                dve.wait_ge(s_free, FROM + b)
                dve.wait_ge(s_base, FROM + b * 32)
                dve.wait_ge(s_fev, (b + 1) * NG)
                nc.vector.tensor_tensor(rec[:, :, D:2 * D], hbuf[:, :, :], cen, ALU.add).then_inc(s_h2, 1)
                dve.wait_ge(s_h2, b + 1)

            def second_center(b):
                center(postc.link, rec[:, :, D:2 * D], slice(0, NT)).then_inc(s_cen, 1)

            def second_norm(b):
                dve.wait_ge(s_sq, b + 1)
                normalize(postc.link, slice(0, NT)).then_inc(s_xn2, 1)

            def choose(b):
                link = postc.link
                mx, best = st[:, 8, :], st[:, 9, :]
                dve.wait_ge(s_lg, FROM + b + 1)
                link(nc.vector.tensor_tensor(lg[:, :, :], bank(LOGIT_BANK, NT * E).rearrange("p (t e) -> p t e", e=E),
                                             gbr[:, :].unsqueeze(1).broadcast_to([P, NT, E]), ALU.add))
                link(nc.vector.tensor_reduce(mx, lg[:, :, :], AX_X, ALU.max))
                nc.vector.tensor_tensor(lg[:, :, :], lg[:, :, :], over(mx, E), ALU.subtract).then_inc(s_lmx, 1)
                dve.wait_ge(s_lmx, b + 1)
                link(nc.vector.tensor_scalar(hot[:, :, :], lg[:, :, :], 0.0, float(-E), ALU.is_equal, ALU.mult))
                link(nc.vector.tensor_tensor(hot[:, :, :], eidx[:, 0:NT, :], hot[:, :, :], ALU.add))
                link(nc.vector.tensor_reduce(best, hot[:, :, :], AX_X, ALU.min))
                link(nc.vector.tensor_scalar(best, best, float(E), None, ALU.add))
                link(nc.vector.tensor_tensor(hot[:, :, :], eidx[:, 0:NT, :], over(best, E), ALU.is_equal))
                link(nc.vector.tensor_tensor(hot[:, :, :], hot[:, :, :], over(valid[:, :], E), ALU.mult))
                nc.vector.tensor_copy(hot16[:, :, :], hot[:, :, :]).then_inc(s_hot, 1)

            def place(b):
                link = postc.link
                esum = st[:, 10, :]
                n, tiles, ends, first, glob = em[:, 0, :], em[:, 1, :], em[:, 2, :], em[:, 3, :], em[:, 4, :]
                ones = em[:, 5, :]
                dve.wait_ge(s_lex, b + 1)
                link(nc.vector.tensor_reduce(esum, lex[:, :, :], AX_X, ALU.add))
                link(nc.vector.reciprocal(rec[:, :, COL_P], esum))
                link(nc.vector.tensor_copy(rec[:, :, COL_ID], idf[:, :]))
                link(nc.vector.tensor_scalar(idf[:, :], idf[:, :], float(N), None, ALU.add))

                dve.wait_ge(s_cum, b + 1)
                link(nc.vector.tensor_copy(tot[:, :, 1:NT + 1],
                                           bank(COUNT_BANK)[:, 256:256 + NT * E].rearrange("p (t e) -> p e t", e=E)))
                link(nc.vector.tensor_tensor_scan(pre[:, :, :].rearrange("p e t -> p (e t)"),
                                                  segmul[:, :, :].rearrange("p e t -> p (e t)"),
                                                  tot[:, :, :].rearrange("p e t -> p (e t)"), 0.0,
                                                  ALU.mult, ALU.add))
                link(nc.vector.tensor_tensor(cnt[:, :, :],
                                             bank(COUNT_BANK)[:, 0:NT * E].rearrange("p (t e) -> p t e", e=E),
                                             pre[:, :, 0:NT].rearrange("p e t -> p t e"), ALU.add))
                link(nc.vector.tensor_copy(n, pre[:, :, NT]))
                link(nc.vector.tensor_scalar(tiles, n, 1.0 / P, (P - 1) / P - 0.5 + 0.5 / P, ALU.mult, ALU.add))
                link(nc.vector.tensor_copy(emi[:, :], tiles))
                link(nc.vector.tensor_copy(tiles, emi[:, :]))
                link(nc.vector.memset(ones, 1.0))
                link(nc.vector.tensor_tensor_scan(ends, ones, tiles, 0.0, ALU.mult, ALU.add))
                link(nc.vector.tensor_tensor(first, ends, tiles, ALU.subtract))
                link(nc.vector.tensor_scalar(first, first, float(P), -1.0, ALU.mult, ALU.add))
                link(nc.vector.tensor_tensor(pen[:, :, :], cnt[:, :, :],
                                             seen[:, :].unsqueeze(1).broadcast_to([P, NT, E]), ALU.add))
                link(nc.vector.tensor_scalar(pen[:, :, :], pen[:, :, :], float(CAP), float(PAST_END),
                                             ALU.is_gt, ALU.mult))
                link(nc.vector.tensor_tensor(cnt[:, :, :], cnt[:, :, :],
                                             first.unsqueeze(1).broadcast_to([P, NT, E]), ALU.add))
                link(nc.vector.tensor_tensor(cnt[:, :, :], cnt[:, :, :], pen[:, :, :], ALU.add))
                link(nc.vector.tensor_tensor(cnt[:, :, :], cnt[:, :, :], hot[:, :, :], ALU.mult))
                link(nc.vector.tensor_reduce(slotf[:, :], cnt[:, :, :], AX_X, ALU.add))
                link(nc.vector.tensor_tensor(slotf[:, :], slotf[:, :], pastend[:, :], ALU.add))
                nc.vector.tensor_copy(slot[:, :], slotf[:, :]).then_inc(s_slot, 1)
                link(nc.vector.tensor_tensor(seen[:, :], seen[:, :], n, ALU.add))
                link(nc.vector.tensor_tensor(ehot[:, :, :], tileno[:, :, :],
                                             ends.unsqueeze(1).broadcast_to([P, FT, E]), ALU.is_ge))
                link(nc.vector.tensor_reduce(ejf[:, :], ehot[:, :, :], AX_X, ALU.add))
                link(nc.vector.tensor_scalar(ejf[:, :], ejf[:, :], float(E - 1), None, ALU.min))
                link(nc.vector.tensor_tensor(ehot[:, :, :], eidx[:, :, :], over(ejf[:, :], E), ALU.is_equal))
                for f in range(NF):
                    link(nc.vector.tensor_tensor(eprod[:, :, :], ehot[:, :, :],
                                                 fb1c[:, :, f].unsqueeze(1).broadcast_to([P, FT, E]), ALU.mult))
                    link(nc.vector.tensor_reduce(fbias[:, f, :], eprod[:, :, :], AX_X, ALU.add))
                nc.vector.tensor_copy(ej[:, :], ejf[:, :]).then_inc(s_ej, 1)

            def mix(b, post, tok):
                t = b + 1
                tokc.at(t)
                postc.at(b)
                if post:
                    residual(b)
                for c in range(NCH):
                    if tok:
                        products(t, c)
                    if post and c == 0:
                        second_center(b)
                    if post and c == 1:
                        second_norm(b)
                    if tok and c == 3:
                        add_bias(t, 0)
                    if post and c == 4:
                        choose(b)
                        dve.wait_ge(s_rl, b + 1)
                    if tok and c == 5:
                        add_bias(t, 1)
                        first_norm(t, 0)
                if tok:
                    low_parts(t, 0)
                    add_bias(t, 2)
                    add_bias(t, 3)
                    first_norm(t, 1)
                    low_parts(t, 1)
                    tokc.ends()
                if post:
                    place(b)
                    postc.ends()

            def attention_round(b, p):
                base = b * STEPS + p * ROUND
                for g in range(ROUND):
                    dve.wait_ge(s_exp, base + (g + 1))
                    dve.wait_ge(s_pv, FROM + base + max(g - HR + 1, 0))
                    if not twice(g):
                        nc.vector.tensor_copy(eh[:, g % HR, :], e32[:, g % ER, :]).then_inc(s_eh, 1)
                        dve.wait_ge(s_eh, b * (2 * CASTS) + p * CASTS + casts(g + 1))
                    nc.vector.tensor_tensor(el[:, g % HR, :], e32[:, g % ER, :], eh[:, g % HR, :],
                                            ALU.subtract).then_inc(s_el, 1)

            def expert_round(i, p):
                expc.at(i * 2 + p)
                link = expc.link
                for r in range(2):
                    for t in range(GT):
                        q = t // 2
                        dve.wait_ge(f_m, i * (FT // 2) + p * GT + (r * (GT // 2) + q + 1))
                        ins = nc.vector.tensor_scalar(fh[:, q % 2, 1, P * (t % 2):P * (t % 2) + P],
                                                      bank(FH_BANK[q % 2][1])[:, P * (t % 2):P * (t % 2) + P],
                                                      fbias[:, 1, bass.ds(p * (2 * GT) + r * GT + t, 1)], 0.0,
                                                      ALU.add, ALU.max)
                        if t % 2:
                            ins.then_inc(f_mb, 1)
                for r in range(2):
                    fz3 = fz[:, r, :].rearrange("p (g d) -> p g d", d=D)
                    fo3 = fo[:, r, :].rearrange("p (g d) -> p g d", d=D)
                    link(nc.vector.tensor_scalar(fstale[:, r, :], frec[:, r, :, COL_ID], oldest[:, :],
                                                 float(PAST_END), ALU.is_lt, ALU.mult))
                    dve.wait_ge(f_free, i * 4 + p * 2 + (r + 1))
                    link(nc.vector.tensor_tensor(fidx[:, r, :], fstale[:, r, :], frec[:, r, :, COL_ID], ALU.add))
                    dve.wait_ge(f_ye, i * 4 + p * 2 + (r + 1))
                    link(nc.vector.tensor_tensor(fz3, fz3, frec[:, r, :, COL_P:COL_P + 1].broadcast_to([P, GT, D]),
                                                 ALU.mult))
                    link(nc.vector.tensor_scalar(fmask, fz[:, r, :], 0.0, 0.0, ALU.mult, ALU.is_equal))
                    link(nc.vector.tensor_tensor(fnan, fz[:, r, :], fz[:, r, :], ALU.not_equal))
                    link(nc.vector.tensor_scalar(fo[:, r, :], fz[:, r, :], -1e4, 1e4, ALU.max, ALU.min), apart=True)
                    link(nc.vector.copy_predicated(fo[:, r, :], fmask, fz[:, r, :]), apart=True)
                    link(nc.vector.copy_predicated(fo[:, r, :], fnan, zero[:, :]))
                    nc.vector.tensor_tensor(fo3, fo3, frec[:, r, :, D:2 * D], ALU.add).then_inc(f_o, 1)
                expc.ends()

            def next_oldest(i):
                dve.wait_ge(f_o, FROM2 + i * 4 + 4)
                nc.vector.tensor_scalar(oldest[:, :], oldest[:, :], float(N), None, ALU.add).then_inc(s_old, 1)
                dve.wait_ge(s_old, i + 1)

            def attend(b):
                with dve.Fori(0, 2) as p:
                    attention_round(b, p)
                    expert_round(b, p)
                next_oldest(b)

            mix(-1, False, True)
            with dve.Fori(0, B - 1) as b:
                attend(b)
                mix(b, True, True)
            attend(B - 1)
            mix(B - 1, True, False)
            with dve.Fori(0, 2) as p:
                expert_round(B, p)


_INS = ['x', 'cls_tok', 'L0_tok_W1', 'L0_tok_b1', 'L0_tok_W2', 'L0_tok_b2', 'L0_tok_W3', 'L0_tok_b3',
        'L0_ffn_gate_w', 'L0_ffn_gate_b', 'L0_ffn_w1', 'L0_ffn_b1', 'L0_ffn_w2', 'L0_ffn_b2']


def kernel(**inputs):
    import numpy as _np
    import concourse.bacc as _bacc
    from concourse import mybir as _mybir
    from concourse.bass_utils import run_bass_kernel_spmd as _run

    nc = _bacc.Bacc("TRN2", target_bir_lowering=False, num_devices=1)
    arrays, args = {}, []
    for name in _INS:
        a = _np.ascontiguousarray(inputs[name])
        arrays[f"in_{name}_dram"] = a
        args.append(nc.dram_tensor(f"in_{name}_dram", a.shape, _mybir.dt.from_np(a.dtype), kind="ExternalInput").ap())
    B, C, H, W = inputs["x"].shape
    args.append(nc.dram_tensor("out_0_dram", (B, H * W + 1, C), _mybir.dt.float32, kind="ExternalOutput").ap())
    vit_block_kernel(nc, *args)
    r = _run(nc, [arrays], core_ids=[0])
    return r.results[0]["out_0_dram"]
```

```python
from contextlib import ExitStack

import concourse.bass as bass
from concourse import mybir

P = 128
ALU = mybir.AluOpType
ACT = mybir.ActivationFunctionType
F32 = mybir.dt.float32
F16 = mybir.dt.float16
BF16 = mybir.dt.bfloat16
I32 = mybir.dt.int32
U32 = mybir.dt.uint32
AX_X = mybir.AxisListType.X
LN_EPS = 1e-5
RSQRT_MAGIC = 0x5F3759DF
NEWTON = 3
PAST_END = 1 << 23
FROM = 1
FROM2 = 2


class Chain:

    def __init__(self, eng, sem, settled, per=0):
        self.eng, self.sem, self.settled, self.per = eng, sem, settled, per
        self.base, self.n = 0, 0

    def at(self, turn, n=0):
        self.base, self.n = turn * self.per, n

    def link(self, ins, apart=False):
        self.n += 1
        ins.then_inc(self.sem, 1)
        self.eng.wait_ge(self.sem, self.base + self.n)
        if apart:
            self.eng.sem_inc(self.settled, 1)

    def ends(self):
        assert self.n == self.per, (self.n, self.per)


def vit_block_kernel(nc, x, cls_tok, W1, b1, W2, b2, W3, b3, gate_w, gate_b, w1, fb1, w2, fb2, out):
    B, C, H, W = x.shape
    HW = H * W
    N = HW + 1
    D = C
    TAPS = 9
    E, _, FF = w1.shape
    T = B * N
    CAP = max(1, -(-5 * T // (4 * E)))
    NT = -(-N // P)
    NP = NT * P
    TAIL = N - (NT - 1) * P
    PW = W + 2
    PH = H + 2

    CROWS = 8
    NCH = H // CROWS
    assert 3 * CROWS + 2 <= H // 2
    CN = CROWS * W
    PAIRS = [(0, 3), (1, 4), (2, 5), (6, 7), (8, None)]
    WINDOW = [(0, 0, 0), (0, 0, 1), (0, 0, 2), (1, 2, 0), (0, 2, 2)]
    KT = len(PAIRS)
    TH = 4
    HALVES = 2
    HROWS = H // HALVES
    PADS = 4 * HALVES

    NU = 4
    UQ = -(-N // NU)
    QA = (UQ + 1) // 2
    QB = UQ - QA
    QPAD = NU * UQ - N
    LAG = 3
    ER = 3
    HR = 4
    STEPS = NU * NT

    def twice(g):
        return g % 5 in (1, 3)

    def casts(g):
        return sum(not twice(k) for k in range(g))

    CASTS = casts(STEPS)

    FT = (N + E * (P - 1)) // P
    GT = 8
    HT = 2 * GT
    assert FT == 2 * HT
    LT = 3 * HT
    FINISH = 9
    RLAG = 2
    TURN_STEPS = (15, 33, 51, 70)
    HIDDEN_STEPS = tuple(range(s + 2, s + 2 + 2 * GT, 2) for s in TURN_STEPS)
    FINISH_STEPS = tuple(range(s + 19, s + 19 + FINISH) for s in TURN_STEPS)
    NF = FF // P
    WP = 3
    REC = 2 * D + 4
    COL_P = 2 * D
    COL_ID = 2 * D + 1

    NG = -(-NT // 8)
    assert NT % 2 == 1
    NGR = -(-NT // 8)
    NORM = (slice(0, 8), slice(8, 16), slice(16, NT))
    NPART = len(NORM)
    TURN_PART = (0, 1, 2, 2)
    NORM_STEPS = (2, 3, 4, 5)
    HIGH_STEP, LOW_STEP = 7, 8
    LATE_TURN = {2: 1, 10: 2, 12: 3}
    KEYS_AT = {8: 4, 15: 8}
    EARLY_CONV = {STEPS - 3: 0, STEPS: 1}
    EARLY_LOGITS = STEPS + 1

    recs = nc.dram_tensor("expert_records", (FT * P, REC), F32, kind="Internal").ap()
    out_rows = out.rearrange("b n d -> (b n) d")

    def group(j, size=8):
        return range(size * j, min(size * j + size, NT))

    def span(j, size=8):
        return slice(size * j, min(size * j + size, NT))

    def tiles_after(c):
        return NT if c == NCH - 1 else (1 + CN * (c + 1)) // P

    with ExitStack() as ctx:
        def sb(name, shape, dt=F32):
            return ctx.enter_context(nc.sbuf_tensor(name, shape, dt))

        def sem(name):
            return ctx.enter_context(nc.semaphore(name))

        ps = ctx.enter_context(nc.psum_tensor("ps", [P, 8 * 512], F32))

        def bank(k, n=512):
            return ps[:, 512 * k:512 * k + n]

        def pair(k):
            return ps[:, 512 * (k + 1) - QA:512 * (k + 1) + QB]

        def halves(k):
            return (ps[:, 512 * (k + 1) - QA:512 * (k + 1)], 0, QA), (ps[:, 512 * (k + 1):512 * (k + 1) + QB], QA, QB)

        TAP_BANKS = 2
        SUM_BANK = 2
        TOKEN_BANK = (4, 5)
        CONV_BANK = 6
        FOLD_BANK = (3, 7, 4, 5)
        ROUTER_BANK = (3, 7)
        LOGIT_BANK = 3
        COUNT_BANK = 7
        TURN_BANK = ((3, 6), (6, 7), (6, 7), (6, 7))
        FH_BANK, FY_BANK = 6, 7
        LAST_FH_BANK = (0, 1)

        w1p = sb("w1p", [P, KT, C])
        w2p = sb("w2p", [C, KT, P])
        w3p = sb("w3p", [P, KT, C])
        b1c = sb("b1c", [C, 1])
        b2c = sb("b2c", [P, KT])
        b3r = sb("b3r", [P, C])
        bias_first = sb("bias_first", [P, C])
        bias_last = sb("bias_last", [P, C])
        gw = sb("gw", [P, 2 * E])
        gbr = sb("gbr", [P, E])
        fw1 = sb("fw1", [P, WP, E * FF], BF16)
        fw2 = sb("fw2", [P, E * NF * D])
        fb1c = sb("fb1c", [P, E, NF])
        fb2p = sb("fb2p", [WP, E * D], BF16)
        ident = sb("ident", [P, P])
        ident16 = sb("ident16", [P, P], F16)
        fold = sb("fold", [P, D])
        tri = sb("tri", [P, P], F16)
        ones16 = sb("ones16", [P, P], F16)
        ones3 = sb("ones3", [WP, P], BF16)
        eidx = sb("eidx", [P, FT, E])
        tileno = sb("tileno", [P, FT, E])
        segmul = sb("segmul", [P, E, NT + 1])
        valid = sb("valid", [P, NT])
        pastend = sb("pastend", [P, NT])
        idf = sb("idf", [P, NT])
        oldest = sb("oldest", [P, 3])
        fillrec = sb("fillrec", [P, REC])
        zero = sb("zero", [P, GT * D])

        xs = sb("xs", [P, HROWS * W])
        xpa = sb("xpa", [P, PH, PW])
        xpb = sb("xpb", [P, PH, PW])
        h1 = sb("h1", [C, 2, CN])
        th = sb("th", [P, TH, CN])
        FLAT = 8960
        flat = sb("flat", [P, FLAT])
        hbuf = sb("hbuf", [P, NT, D])
        st = sb("st", [P, 12, NT])
        v3 = sb("v3", [P, NT, 3 * D], F16)
        kA = sb("kA", [P, NP], F16)
        kB = sb("kB", [P, NP], F16)
        ctxT = sb("ctxT", [P, NP])
        rs = sb("rs", [P, NT, NU])
        rec = sb("rec", [P, NT, REC])
        rec16 = rec[:, :, 0:D].bitcast(F16)
        lg = sb("lg", [P, NT, E])
        lex = sb("lex", [P, NT, E])
        cnt = sb("cnt", [P, NT, E])
        pen = sb("pen", [P, NT, E])
        hot = sb("hot", [P, NT, E])
        hot16 = sb("hot16", [P, NT, E], F16)
        tot = sb("tot", [P, E, NT + 1])
        pre = sb("pre", [P, E, NT + 1])
        seen = sb("seen", [P, E])
        em = sb("em", [P, 5, E])
        emi = sb("emi", [P, E], I32)
        slotf = sb("slotf", [P, NT])
        slot = sb("slot", [P, NT], I32)
        ehot = sb("ehot", [P, FT, E])
        eprod = sb("eprod", [P, FT, E])
        ejf = sb("ejf", [P, FT])
        ej = sb("ej", [P, LT], I32)
        fbias = sb("fbias", [P, NF, LT])

        HALF = (HR * UQ + 1) // 2
        att = sb("att", [P, ER * UQ + 2 * HALF])
        e32 = att[:, 0:ER * UQ].rearrange("p (r n) -> p r n", r=ER)
        eh = att[:, ER * UQ:ER * UQ + HALF].bitcast(F16)[:, 0:HR * UQ].rearrange("p (r n) -> p r n", r=HR)
        el = att[:, ER * UQ + HALF:ER * UQ + 2 * HALF].bitcast(F16)[:, 0:HR * UQ].rearrange("p (r n) -> p r n", r=HR)
        cen = att[:, 0:NT * D].rearrange("p (t d) -> p t d", d=D)
        sqr = att[:, NT * D:2 * NT * D].rearrange("p (t d) -> p t d", d=D)
        xnT = att[:, 2 * NT * D:2 * NT * D + 2 * 4 * P].rearrange("p (r n) -> p r n", r=2)
        assert 2 * NT * D + 2 * 4 * P <= ER * UQ + 2 * HALF

        frec = sb("frec", [P, 2, GT, REC])
        frec16 = frec[:, :, :, 0:D].bitcast(F16)
        fo = sb("fo", [P, 2, GT * D])
        fstale = sb("fstale", [P, 2, GT])
        fidx = sb("fidx", [P, 2, GT], I32)

        prod = flat[:, 0:2 * KT * CN].rearrange("p (a k n) -> p a k n", a=2, k=KT)
        SUMS = 2 * KT * CN
        sums = flat[0:D, SUMS:SUMS + NP]
        LATE = SUMS + NP
        fx = flat[:, 0:GT * P].bitcast(F16).rearrange("p (r n) -> p r n", r=2)
        fh = flat[:, 1024:1024 + 2 * NF * P].rearrange("p (r f n) -> p r f n", r=2, f=NF)
        fz = flat[:, 2048:2048 + 2 * GT * D].rearrange("p (r n) -> p r n", r=2)
        fmask = flat[:, 3072:3072 + GT * D].bitcast(I32)
        fnan = flat[:, 3584:3584 + GT * D].bitcast(I32)

        ncen = (cen[:, NORM[0], :], flat[:, LATE:LATE + 8 * D].rearrange("p (t d) -> p t d", d=D),
                flat[:, 1024:1024 + (NT - 16) * D].rearrange("p (t d) -> p t d", d=D))
        nsqr = (sqr[:, NORM[0], :], flat[:, LATE + 8 * D:LATE + 16 * D].rearrange("p (t d) -> p t d", d=D),
                flat[:, 1700:1700 + (NT - 16) * D].rearrange("p (t d) -> p t d", d=D))

        w1f = flat[:, 0:TAPS * C].rearrange("p (k o) -> p k o", k=TAPS)
        w2f = flat[0:C, 600:600 + TAPS * C]
        b2f = flat[:, 1200:1200 + TAPS]
        clsr = flat[0:1, 1220:1220 + C]
        fw1f = flat[:, 1300:1300 + E * FF]
        fw1r = flat[:, 3400:3400 + E * FF]
        fb2f = flat[0:WP, 5500:5500 + E * D]
        fb2s = flat[0:WP, 6100:6100 + E * D]
        fb2b = flat[0:WP, 6700:6700 + E * D // 2].bitcast(BF16)
        gwf = flat[:, 7000:7000 + E]
        assert max(3400 + E * FF, LATE + 16 * D) <= FLAT

        s_w = sem("weights_loaded")
        s_cst = sem("constants_made")
        s_wp = sem("weights_packed")
        s_fill = sem("records_filled")
        s_settled = sem("settled")
        s_pool = sem("pool_chain")
        s_old = sem("oldest_row_moved")
        s_dw = sem("vector_weights_chain")
        s_dt = sem("vector_token_chain")
        s_dn = sem("vector_norm_chain")
        s_dp = sem("vector_post_chain")
        s_df = sem("vector_expert_chain")
        s_x = sem("image_loaded")
        s_pad = sem("image_padded")
        s_conv = sem("conv_done")
        s_h1 = sem("h1_ready")
        s_z2 = sem("tap_logits_ready")
        s_th = sem("tap_gates_ready")
        s_prod = sem("products_ready")
        s_tk = sem("products_used")
        s_sum = sem("sums_evacuated")
        s_w3 = sem("tokens_turned")
        s_hev = sem("tokens_evacuated")
        s_xn = sem("normed_ready")
        s_vh = sem("high_parts_ready")
        s_v3 = sem("low_parts_ready")
        s_ta = sem("parts_transposed")
        s_ka = sem("keys_ready")
        s_sc = sem("scores_ready")
        s_exp = sem("exp_ready")
        s_eh = sem("exp_high_ready")
        s_el = sem("exp_low_ready")
        s_pv = sem("exp_parts_used")
        s_cev = sem("context_evacuated")
        s_fold = sem("context_folded")
        s_fev = sem("folded_evacuated")
        s_h2 = sem("residual_ready")
        s_cen = sem("centered_ready")
        s_sq = sem("squares_ready")
        s_xn2 = sem("second_normed_ready")
        s_rh = sem("record_high_ready")
        s_rl = sem("record_low_ready")
        s_gt = sem("router_input_transposed")
        s_gte = sem("router_input_evacuated")
        s_gl = sem("router_input_used")
        s_lg = sem("router_logits_ready")
        s_lmx = sem("router_shifted")
        s_lex = sem("router_exp_ready")
        s_hot = sem("choice_ready")
        s_cum = sem("counts_ready")
        s_slot = sem("slots_ready")
        s_ej = sem("tile_experts_ready")
        s_base = sem("plain_rows_written")
        s_scat = sem("records_scattered")
        s_free = sem("record_buffer_free")
        f_ld = [sem("group_loaded_0"), sem("group_loaded_1")]
        f_t = sem("group_transposed")
        f_te = sem("group_evacuated")
        f_m = sem("hidden_ready")
        f_ma = sem("hidden_evacuated")
        f_y = sem("expert_out_ready")
        f_ye = sem("expert_out_evacuated")
        f_o = sem("result_ready")
        f_st = [sem("result_written_0"), sem("result_written_1")]
        f_free = sem("result_buffer_free")

        def settle(eng):
            eng.sem_inc(s_settled, 1)

        block = ctx.enter_context(nc.Block())
        N_LOADS = 8 + 2 * KT - 1 + 3 + 6

        @block.sync
        def _(sp):
            n = [0]
            sp.sem_inc(s_base, FROM)

            def load(dst, src):
                n[0] += 1
                sp.dma_start(dst, src).then_inc(s_w, 16)

            w1v = W1.rearrange("(c k) o -> c k o", k=TAPS)
            w3v = W3.rearrange("(c k) o -> c k o", k=TAPS)
            b2v = b2.rearrange("(c k) -> c k", k=TAPS)
            for a in range(2):
                load(w1f[C * a:C * a + C, :, :], w1v)
                load(b2f[C * a:C * a + C, :], b2v)
            load(b1c[:, :], b1.rearrange("(c a) -> c a", a=1))
            load(w2f, W2)
            load(b3r[:, :], b3.partition_broadcast(P))
            load(clsr, cls_tok.rearrange("a b d -> (a b) d"))
            for kt, (ka, kb) in enumerate(PAIRS):
                load(w3p[0:C, kt, :], w3v[:, ka, :])
                if kb is not None:
                    load(w3p[C:P, kt, :], w3v[:, kb, :])
            for a in range(2):
                load(gwf[D * a:D * a + D, :], gate_w)
            load(gbr[:, :], gate_b.partition_broadcast(P))
            load(fb2f, fb2.rearrange("e d -> (e d)").partition_broadcast(WP))
            for a in range(2):
                load(fw1f[D * a:D * a + D, :].rearrange("p (e f) -> p e f", e=E), w1.rearrange("e d f -> d e f"))
            load(fw2[:, :].rearrange("p (e d) -> p e d", d=D), w2.rearrange("e (f p) d -> p (e f) d", p=P))
            with nc.allow_non_contiguous_dma("8 KB of biases, one column each"):
                for f in range(NF):
                    load(fb1c[:, :, f], fb1[:, P * f:P * f + P].rearrange("e p -> p e"))
            assert n[0] == N_LOADS, n

            def write_rows(b):
                sp.wait_ge(s_h2, b + 1)
                sp.dma_start(out[bass.ds(b, 1), 0:(NT - 1) * P, :].rearrange("a (t p) d -> p (a t) d", p=P),
                             rec[:, 0:NT - 1, D:2 * D]).then_inc(s_base, 16)
                sp.dma_start(out[bass.ds(b, 1), (NT - 1) * P:N, :].rearrange("a p d -> (a p) d"),
                             rec[0:TAIL, NT - 1, D:2 * D]).then_inc(s_base, 16)

            def load_pair(first, half):
                for r in range(2):
                    sp.wait_ge(f_o, first + (r + 1))
                    g = 2 * half + r
                    sp.dma_start(frec[:, r, :, :],
                                 recs[P * GT * g:P * GT * (g + 1), :].rearrange("(g p) c -> p g c", p=P)
                                 ).then_inc(f_ld[r], 16)

            sp.wait_ge(s_fill, 16)
            load_pair(0, 1)
            load_pair(2, 0)
            load_pair(4, 1)
            write_rows(0)
            with sp.Fori(1, B) as b:
                sp.wait_ge(s_scat, b * (16 * NT))
                load_pair(b * 4 + 2, 0)
                load_pair(b * 4 + 4, 1)
                write_rows(b)
            sp.wait_ge(s_scat, B * (16 * NT))
            load_pair(B * 4 + 2, 0)
            load_pair(B * 4 + 4, 1)

        @block.gpsimd
        def _(pool):
            chain = Chain(pool, s_pool, s_settled)
            link = chain.link
            pool.sem_inc(s_free, FROM)
            pool.sem_inc(f_free, FROM2)

            def load_half(b, hf):
                r0 = hf * HROWS
                for a in range(2):
                    pool.dma_start(xs[C * a:C * a + C, :],
                                   x[bass.ds(b, 1), :, r0:r0 + HROWS, :].rearrange("a c h w -> (a c) (h w)")
                                   ).then_inc(s_x, 16)

            link(nc.gpsimd.memset(fillrec[:, :], 0.0))
            link(nc.gpsimd.memset(fillrec[:, COL_ID:COL_ID + 1], float(PAST_END)))
            pool.dma_start(recs.rearrange("(p r) c -> p r c", p=P),
                           fillrec[:, :].unsqueeze(1).broadcast_to([P, FT, REC])).then_inc(s_fill, 16)

            load_half(0, 0)
            for t, v in ((xpa, 0.0), (xpb, 0.0), (ident, 0.0), (fold, 0.0), (tri, 1.0), (valid, 1.0),
                         (pastend, 0.0), (oldest, float(-N))):
                link(nc.gpsimd.memset(t[tuple(slice(None) for _ in t.shape)], v))
            link(nc.gpsimd.memset(oldest[:, 0:1], float(-2 * N)))
            link(nc.gpsimd.affine_select(out=ident[:, :], in_=ident[:, :], compare_op=ALU.not_equal, fill=1.0,
                                         base=0, pattern=[[-1, P]], channel_multiplier=1))
            for a in range(2):
                link(nc.gpsimd.affine_select(out=fold[:, :], in_=fold[:, :], compare_op=ALU.not_equal, fill=1.0,
                                             base=-D * a, pattern=[[-1, D]], channel_multiplier=1))
            link(nc.gpsimd.affine_select(out=tri[:, :], in_=tri[:, :], compare_op=ALU.is_ge, fill=0.0,
                                         base=0, pattern=[[1, P]], channel_multiplier=-1))
            for t, v in ((valid, 0.0), (pastend, float(PAST_END))):
                link(nc.gpsimd.affine_select(out=t[:, NT - 1:NT], in_=t[:, NT - 1:NT], compare_op=ALU.is_ge,
                                             fill=v, base=TAIL - 1, pattern=[[0, 1]], channel_multiplier=-1))
            link(nc.gpsimd.iota(eidx[:, :, :], pattern=[[0, FT], [1, E]], base=0, channel_multiplier=0,
                                allow_small_or_imprecise_dtypes=True))
            link(nc.gpsimd.iota(tileno[:, :, :], pattern=[[1, FT], [0, E]], base=0, channel_multiplier=0,
                                allow_small_or_imprecise_dtypes=True))
            link(nc.gpsimd.iota(idf[:, :], pattern=[[P, NT]], base=0, channel_multiplier=1,
                                allow_small_or_imprecise_dtypes=True))
            nc.gpsimd.tensor_copy(ident16[:, :], ident[:, :]).then_inc(s_cst, 1)
            pool.wait_ge(s_cst, 1)

            def pad_image(b, loaded=False):
                for hf in range(HALVES):
                    r0 = hf * HROWS
                    if hf or not loaded:
                        load_half(b, hf)
                    pool.wait_ge(s_x, (b * HALVES + (hf + 1)) * 32)
                    settle(pool)
                    img = xs[:, :].rearrange("p (h w) -> p h w", w=W)
                    copies = ((xpa[0:C, 1 + r0:1 + r0 + HROWS, 1:1 + W], img[0:C]),
                              (xpa[C:P, r0:r0 + HROWS, 1:1 + W], img[C:P]),
                              (xpb[0:C, 1 + r0:1 + r0 + HROWS, 1:1 + W], img[0:C]),
                              (xpb[C:P, 1 + r0:1 + r0 + HROWS, 0:W], img[C:P]))
                    for n, (dst, src) in enumerate(copies):
                        nc.gpsimd.tensor_copy(dst, src).then_inc(s_pad, 1)
                        pool.wait_ge(s_pad, b * PADS + (4 * hf + n + 1))
                        settle(pool)

            def record_low(b):
                pool.wait_ge(s_rh, b + 1)
                settle(pool)
                nc.gpsimd.tensor_tensor(rec16[:, :, D:2 * D], sqr, rec16[:, :, 0:D], ALU.subtract).then_inc(s_rl, 1)
                pool.wait_ge(s_rl, b + 1)
                settle(pool)

            def scatter_image(b):
                for r in range(2):
                    pool.wait_ge(f_ld[r], b * 32 + 48)
                pool.wait_ge(s_slot, FROM + b + 1)
                settle(pool)
                for t in range(NT):
                    nc.gpsimd.indirect_dma_start(
                        recs, bass.IndirectOffsetOnAxis(slot[:, t:t + 1].bitcast(U32), 0), rec[:, t, :], None,
                        bounds_check=FT * P - 1, oob_is_err=False).then_inc(s_scat, 16)
                pool.wait_ge(s_scat, (b + 1) * (16 * NT))
                pool.sem_inc(s_free, 1)

            def scatter_pair(i, p):
                for r in range(2):
                    pool.wait_ge(f_o, FROM2 + i * 4 + (2 * p + r + 1))
                    settle(pool)
                    for t in range(GT):
                        nc.gpsimd.indirect_dma_start(
                            out_rows, bass.IndirectOffsetOnAxis(fidx[:, r, t:t + 1].bitcast(U32), 0),
                            fo[:, r, D * t:D * t + D], None,
                            bounds_check=T - 1, oob_is_err=False).then_inc(f_st[r], 16)
                    pool.wait_ge(f_st[r], i * (32 * GT) + 16 * GT * (p + 1))
                    pool.sem_inc(f_free, 1)

            def scatter_results(i):
                pool.wait_ge(s_base, FROM + i * 32)
                scatter_pair(i, 0)
                scatter_pair(i, 1)

            pad_image(0, loaded=True)
            with pool.Fori(0, B - 1) as b:
                pool.wait_ge(s_conv, (b + 1) * NCH)
                pool.wait_ge(s_prod, (b + 1) * (NCH * KT))
                settle(pool)
                pad_image(b + 1)
                scatter_results(b)
                record_low(b)
                scatter_image(b)
            scatter_results(B - 1)
            record_low(B - 1)
            scatter_image(B - 1)
            scatter_results(B)
            scatter_pair(B, 2)

        @block.tensor
        def _(pe):
            for start in (s_pv, s_lg):
                pe.sem_inc(start, FROM)

            def conv(t, c):
                if c >= 1:
                    pe.wait_ge(s_h1, t * NCH + c)
                for kt, (which, r, q) in enumerate(WINDOW):
                    src = (xpa, xpb)[which][:, r + CROWS * c:r + CROWS * (c + 1), q:q + W]
                    last = nc.tensor.matmul(bank(CONV_BANK, CN)[0:C], w1p[:, kt, :], src,
                                            start=kt == 0, stop=kt == KT - 1)
                last.then_inc(s_conv, 1)

            def tap_logits(t, c):
                pe.wait_ge(s_h1, t * NCH + (c + 1))
                for kt in range(KT):
                    n = c * KT + kt
                    if n >= TAP_BANKS:
                        pe.wait_ge(s_th, t * (NCH * KT) + (n - TAP_BANKS + 1))
                    nc.tensor.matmul(bank(n % TAP_BANKS, CN), w2p[:, kt, :], h1[:, c % 2, :],
                                     start=True, stop=True).then_inc(s_z2, 1)

            def token_sums(t, c):
                pe.wait_ge(s_prod, t * (NCH * KT) + KT * (c + 1))
                if c >= 1:
                    pe.wait_ge(s_sum, t * NCH + c)
                for kt in range(KT):
                    last = nc.tensor.matmul(bank(SUM_BANK, CN)[0:D], w3p[:, kt, :], prod[:, c % 2, kt, :],
                                            start=kt == 0, stop=kt == KT - 1)
                last.then_inc(s_tk, 1)

            def turn_tokens(t, c):
                pe.wait_ge(s_sum, t * NCH + (c + 1))
                settle(pe)
                for k in range(tiles_after(c - 1) if c else 0, tiles_after(c)):
                    j = k // 8
                    if k % 8 == 0 and j >= 2:
                        pe.wait_ge(s_hev, t * NG + (j - 1))
                        settle(pe)
                    last = nc.tensor.transpose(bank(TOKEN_BANK[j % 2])[:, D * (k % 8):D * (k % 8 + 1)],
                                               sums[:, P * k:P * k + P], ident[0:D, 0:D])
                    if k % 8 == 7 or k == NT - 1:
                        last.then_inc(s_w3, 1)

            def turn(t, j):
                pe.wait_ge(s_v3, t * NPART + TURN_PART[j] + 1)
                if j >= 2:
                    pe.wait_ge(s_ka, t * (2 * NG) + 2 * j)
                for a in range(2):
                    dst = bank(TURN_BANK[j][a]).bitcast(F16)
                    for i, k in enumerate(group(j)):
                        last = nc.tensor.transpose(dst[:, P * i:P * i + P], v3[:, k, D * a:D * a + 2 * D],
                                                   ident16[:, :])
                    last.then_inc(s_ta, 1)

            def turn_records(i, p, r):
                if r == 0:
                    pe.wait_ge(s_ej, FROM + i)
                    settle(pe)
                pe.wait_ge(f_ld[r], i * 32 + (p * 16 + 16))
                settle(pe)
                dst = bank(FH_BANK).bitcast(F16)
                for t in range(GT):
                    last = nc.tensor.transpose(dst[:, P * t:P * t + P], frec16[:, r, t, :], ident16[:, :])
                last.then_inc(f_t, 1)
                return nc.values_load_multi_w_load_instructions(
                    ej[0:1, bass.ds(p * HT + r * GT, GT)], engines=[pe.engine], min_val=0, max_val=E - 1,
                    skip_runtime_bounds_check_because="clamped on the chip to 0..E-1")[1]

            def hidden(i, p, r, t, expert, at=FH_BANK):
                if t == 0:
                    pe.wait_ge(f_te, i * 4 + p * 2 + (r + 1))
                for f in range(NF):
                    for w in range(WP):
                        last = nc.tensor.matmul(bank(at)[:, P * f:P * f + P],
                                                fw1[:, w, bass.ds(expert * FF + P * f, P)],
                                                fx[:, r, P * t:P * t + P], start=w == 0, stop=w == WP - 1)
                last.then_inc(f_m, 1)

            def result(i, p, r, t, expert):
                pe.wait_ge(f_ma, i * FT + p * HT + (r * GT + t + 1))
                if t == 0:
                    pe.wait_ge(f_ye, FROM + i * 4 + (p * 2 + r))
                dst = bank(FY_BANK)[:, D * t:D * t + D]
                for f in range(NF):
                    nc.tensor.matmul(dst, fh[:, t % 2, f, :], fw2[:, bass.ds(expert * (NF * D) + D * f, D)],
                                     start=f == 0, stop=False)
                last = nc.tensor.matmul(dst, ones3[:, :], fb2p[:, bass.ds(expert * D, D)], start=False, stop=True)
                if t == GT - 1:
                    last.then_inc(f_y, 1)

            def attention(b, more):
                base = b * STEPS
                pe.wait_ge(s_ka, b * (2 * NG) + 2)
                settle(pe)
                for g in range(STEPS + LAG):
                    if g < STEPS:
                        u, m = divmod(g, NT)
                        if g in KEYS_AT:
                            pe.wait_ge(s_ka, b * (2 * NG) + KEYS_AT[g])
                        if g >= 2:
                            pe.wait_ge(s_exp, base + (g - 1))
                        for dst, off, n in halves(2 * (g % 2)):
                            for keys in (kA, kB):
                                last = nc.tensor.matmul(dst, kA[:, P * m:P * m + P],
                                                        keys[:, u * UQ + off:u * UQ + off + n],
                                                        start=keys is kA, stop=keys is kB)
                        last.then_inc(s_sc, 1)
                    if g in LATE_TURN:
                        turn(b, LATE_TURN[g])
                    for q in range(4):
                        if g - RLAG in HIDDEN_STEPS[q]:
                            t = HIDDEN_STEPS[q].index(g - RLAG)
                            result(b, q // 2, q % 2, t, experts[t])
                        if g == TURN_STEPS[q]:
                            experts = turn_records(b, q // 2, q % 2)
                        if g in HIDDEN_STEPS[q]:
                            t = HIDDEN_STEPS[q].index(g)
                            hidden(b, q // 2, q % 2, t, experts[t])
                    if more and g in EARLY_CONV:
                        if EARLY_CONV[g] == 0:
                            pe.wait_ge(s_pad, (b + 1) * PADS + PADS)
                        conv(b + 1, EARLY_CONV[g])
                    if more and g == EARLY_LOGITS:
                        pe.wait_ge(s_exp, base + STEPS)
                        tap_logits(b + 1, 0)
                    if g >= LAG:
                        k = g - LAG
                        u, m = divmod(k, NT)
                        if k == 0:
                            pe.wait_ge(s_hev, (b + 1) * NG)
                        if m == 0:
                            pe.wait_ge(s_cev, FROM + b * NU + u)
                        pe.wait_ge(s_el, FROM + base + (k + 1))
                        for part in (eh, el):
                            for dst, off, n in halves(4):
                                last = nc.tensor.matmul(dst, v3[:, m, 0:2 * D], part[:, k % HR, off:off + n],
                                                        start=m == 0 and part is eh, stop=m == NT - 1 and part is el)
                        last.then_inc(s_pv, 1)

            def last_experts(p):
                for r in range(2):
                    experts = turn_records(B, p, r)
                    hidden(B, p, r, 0, experts[0], LAST_FH_BANK[0])
                    for t in range(GT):
                        if t + 1 < GT:
                            hidden(B, p, r, t + 1, experts[t + 1], LAST_FH_BANK[(t + 1) % 2])
                        result(B, p, r, t, experts[t])

            def fold_context(b):
                pe.wait_ge(s_cev, FROM + (b + 1) * NU)
                pe.wait_ge(f_ye, FROM + b * 4 + 4)
                for j in range(NG):
                    for i, k in enumerate(group(j)):
                        last = nc.tensor.matmul(bank(FOLD_BANK[j])[:, D * i:D * i + D], ctxT[:, P * k:P * k + P],
                                                fold[:, :], start=True, stop=True)
                    last.then_inc(s_fold, 1)

            def turn_router(b, j):
                if j < NGR:
                    if j == 0:
                        pe.wait_ge(s_xn2, b + 1)
                        pe.wait_ge(s_fev, (b + 1) * NG)
                    else:
                        pe.wait_ge(s_gte, b * NGR + j)
                    settle(pe)
                    for i, k in enumerate(group(j)[::2]):
                        if k == NT - 1:
                            last = nc.tensor.transpose(bank(ROUTER_BANK[1])[0:D, P * i:P * i + P], sqr[:, k, :],
                                                       ident[:, :])
                        else:
                            last = nc.tensor.transpose(bank(ROUTER_BANK[1])[:, P * i:P * i + P],
                                                       sqr[:, k:k + 2, :].rearrange("p t d -> p (t d)"),
                                                       ident[:, :])
                    last.then_inc(s_gt, 1)

            def router_logits(b, j):
                pe.wait_ge(s_gte, b * NGR + (j + 1))
                for i, k in enumerate(group(j)[::2]):
                    rows, n = (D, E) if k == NT - 1 else (P, 2 * E)
                    last = nc.tensor.matmul(bank(LOGIT_BANK)[:, E * k:E * k + n], xnT[0:rows, j % 2, P * i:P * i + P],
                                            gw[0:rows, 0:n], start=True, stop=True)
                last.then_inc(s_gl if j < NGR - 1 else s_lg, 1)

            def router_step(b, j):
                turn_router(b, j)
                if j >= 1:
                    router_logits(b, j - 1)

            def count(b):
                pe.wait_ge(s_hot, b + 1)
                hv = hot16[:, :, :].rearrange("p t e -> p (t e)")
                nc.tensor.matmul(bank(COUNT_BANK)[:, 0:NT * E], tri[:, :], hv, start=True, stop=True)
                nc.tensor.matmul(bank(COUNT_BANK)[:, 256:256 + NT * E], ones16[:, :], hv,
                                 start=True, stop=True).then_inc(s_cum, 1)

            def mix(b, post, tok):
                t = b + 1
                if tok and not post:
                    pe.wait_ge(s_pad, t * PADS + PADS // HALVES)
                    conv(t, 0)
                    conv(t, 1)
                steps = {2: ((0,), (1,), (2,)), 3: ((3,), (4,), ())}
                for c in range(NCH):
                    todo = steps.get(c, ((), (), ())) if post else ((), (), ())
                    if tok and c + 2 < NCH:
                        if not post and c == 1:
                            pe.wait_ge(s_pad, t * PADS + PADS)
                        conv(t, c + 2)
                    for j in todo[0]:
                        router_step(b, j)
                    if tok and (c >= 1 or not post):
                        tap_logits(t, c)
                    if post and c == 0:
                        fold_context(b)
                    for j in todo[1]:
                        router_step(b, j)
                    if tok and c:
                        token_sums(t, c - 1)
                    if tok and c >= 2:
                        if post and c == 2:
                            pe.wait_ge(s_fev, (b + 1) * NG)
                        turn_tokens(t, c - 2)
                    for j in todo[2]:
                        router_step(b, j)
                    if post and c == 3:
                        count(b)
                if tok:
                    token_sums(t, NCH - 1)
                    turn(t, 0)
                    turn_tokens(t, NCH - 2)
                    turn_tokens(t, NCH - 1)

            pe.wait_ge(s_cst, 1)
            pe.wait_ge(s_wp, 1)
            mix(-1, False, True)

            with pe.Fori(0, B - 1) as b:
                attention(b, True)
                mix(b, True, True)
            attention(B - 1, False)
            mix(B - 1, True, False)
            with pe.Fori(0, 3) as p:
                last_experts(p)

        @block.scalar
        def _(act):
            for start in (s_cev, f_ye):
                act.sem_inc(start, FROM)

            def relu(t, c):
                act.wait_ge(s_conv, t * NCH + (c + 1))
                if c >= 2:
                    act.wait_ge(s_z2, t * (NCH * KT) + KT * (c - 1))
                nc.scalar.activation(h1[:, c % 2, :], bank(CONV_BANK, CN)[0:C], ACT.Relu,
                                     bias=b1c[:, :]).then_inc(s_h1, 1)

            def tap_gates(t, c):
                for kt in range(KT):
                    n = c * KT + kt
                    act.wait_ge(s_z2, t * (NCH * KT) + (n + 1))
                    if n >= TH:
                        act.wait_ge(s_prod, t * (NCH * KT) + (n - TH + 1))
                    nc.scalar.activation(th[:, n % TH, :], bank(n % TAP_BANKS, CN), ACT.Tanh, scale=0.5,
                                         bias=b2c[:, kt:kt + 1]).then_inc(s_th, 1)

            def sums_out(t, c):
                act.wait_ge(s_tk, t * NCH + (c + 1))
                nc.scalar.copy(sums[:, 1 + CN * c:1 + CN * (c + 1)], bank(SUM_BANK, CN)[0:D]).then_inc(s_sum, 1)

            def high_parts(t, part):
                act.wait_ge(s_xn, t * NPART + (part + 1))
                s = NORM[part]
                n = s.stop - s.start
                nc.scalar.copy(v3[:, s, :].rearrange("p t (a d) -> p t a d", d=D)[:, :, 0:3:2, :],
                               nsqr[part].unsqueeze(2).broadcast_to([P, n, 2, D])).then_inc(s_vh, 1)

            def keys_out(t, j):
                for a, dst in enumerate((kA, kB)):
                    act.wait_ge(s_ta, t * (2 * NG) + (2 * j + a + 1))
                    n = len(group(j)) * P
                    nc.scalar.copy(dst[:, 8 * P * j:8 * P * j + n],
                                   bank(TURN_BANK[j][a]).bitcast(F16)[:, 0:n]).then_inc(s_ka, 1)

            def router_evacuate(b, j):
                act.wait_ge(s_gt, b * NGR + (j + 1))
                if j >= 2:
                    act.wait_ge(s_gl, b * (NGR - 1) + (j - 1))
                rows, n = (D, P) if j == NGR - 1 else (P, 4 * P)
                nc.scalar.copy(xnT[0:rows, j % 2, 0:n], bank(ROUTER_BANK[1], n)[0:rows]).then_inc(s_gte, 1)

            def mix(b, post, tok):
                t = b + 1
                steps = {2: ((0,), (1,), (2,)), 3: ((3,), (), ())}
                if tok and not post:
                    relu(t, 0)
                    relu(t, 1)
                for c in range(NCH):
                    todo = steps.get(c, ((), (), ())) if post else ((), (), ())
                    for j in todo[0]:
                        router_evacuate(b, j)
                    if tok and (c >= 1 or not post):
                        tap_gates(t, c)
                    if post and c == 1:
                        act.wait_ge(s_cen, b + 1)
                        nc.scalar.activation(sqr, cen, ACT.Square).then_inc(s_sq, 1)
                    if tok and c + 2 < NCH:
                        relu(t, c + 2)
                    for j in todo[1]:
                        router_evacuate(b, j)
                    if tok and c:
                        sums_out(t, c - 1)
                    for j in todo[2]:
                        router_evacuate(b, j)
                    if post and c == 1:
                        act.wait_ge(s_xn2, b + 1)
                        nc.scalar.copy(rec16[:, :, 0:D], sqr).then_inc(s_rh, 1)
                    if post and c == 3:
                        act.wait_ge(s_lmx, b + 1)
                        nc.scalar.activation(lex[:, :, :], lg[:, :, :], ACT.Exp).then_inc(s_lex, 1)
                if tok:
                    high_parts(t, 0)
                    keys_out(t, 0)
                    sums_out(t, NCH - 1)

            def records_out(i, p, r):
                act.wait_ge(f_t, i * 4 + p * 2 + (r + 1))
                nc.scalar.copy(fx[:, r, :], bank(FH_BANK).bitcast(F16)).then_inc(f_te, 1)

            def hidden_out(i, p, r, t, at=FH_BANK):
                act.wait_ge(f_m, i * FT + p * HT + (r * GT + t + 1))
                for f in range(NF):
                    last = nc.scalar.activation(fh[:, t % 2, f, :], bank(at)[:, P * f:P * f + P], ACT.Relu,
                                                bias=fbias[:, f, bass.ds(p * HT + r * GT + t, 1)])
                last.then_inc(f_ma, 1)

            def result_out(i, p, r):
                act.wait_ge(f_y, i * 4 + p * 2 + (r + 1))
                nc.scalar.copy(fz[:, r, :], bank(FY_BANK)).then_inc(f_ye, 1)

            def attention(b, more):
                base = b * STEPS

                def context_out(u):
                    act.wait_ge(s_pv, FROM + base + (u + 1) * NT)
                    nc.scalar.copy(ctxT[:, u * UQ:(u + 1) * UQ], pair(4)).then_inc(s_cev, 1)

                high_parts(b, 1)
                for g in range(STEPS):
                    u, m = divmod(g, NT)
                    act.wait_ge(s_sc, base + (g + 1))
                    if twice(g):
                        act.wait_ge(s_pv, FROM + base + max(g - HR + 1, 0))
                        nc.scalar.activation(eh[:, g % HR, :], pair(2 * (g % 2)), ACT.Exp, scale=float(D) ** -0.5)
                    act.wait_ge(s_el, FROM + base + max(g - ER + 1, 0))
                    nc.scalar.activation(e32[:, g % ER, :], pair(2 * (g % 2)), ACT.Exp, scale=float(D) ** -0.5,
                                         accum_out=rs[:, m, u:u + 1]).then_inc(s_exp, 1)
                    if g in LATE_TURN:
                        keys_out(b, LATE_TURN[g])
                    if g == HIGH_STEP:
                        high_parts(b, 2)
                    for q in range(4):
                        if g == TURN_STEPS[q]:
                            records_out(b, q // 2, q % 2)
                        if g in HIDDEN_STEPS[q]:
                            hidden_out(b, q // 2, q % 2, HIDDEN_STEPS[q].index(g))
                        if g == HIDDEN_STEPS[q][-1] + RLAG:
                            result_out(b, q // 2, q % 2)
                    if more and g == STEPS - 3:
                        relu(b + 1, 0)
                    if m == LAG - 1 and u:
                        context_out(u - 1)
                if more:
                    relu(b + 1, 1)
                    tap_gates(b + 1, 0)
                context_out(NU - 1)

            def last_experts(p):
                for r in range(2):
                    records_out(B, p, r)
                    for t in range(GT):
                        hidden_out(B, p, r, t, LAST_FH_BANK[t % 2])
                    result_out(B, p, r)

            act.wait_ge(s_wp, 1)
            act.wait_ge(s_cst, 1)
            mix(-1, False, True)

            with act.Fori(0, B - 1) as b:
                attention(b, True)
                mix(b, True, True)
            attention(B - 1, False)
            mix(B - 1, True, False)
            with act.Fori(0, 3) as p:
                last_experts(p)

        @block.vector
        def _(dve):
            weights = Chain(dve, s_dw, s_settled)
            tokc = Chain(dve, s_dt, s_settled, 17)
            normc = Chain(dve, s_dn, s_settled, 34)
            postc = Chain(dve, s_dp, s_settled, 59)
            expc = Chain(dve, s_df, s_settled, 16)

            def over(v, n, k=None):
                return v.unsqueeze(2).broadcast_to([P, k or v.shape[1], n])

            for start, v in ((s_slot, FROM), (s_el, FROM), (s_ej, FROM), (f_o, FROM2)):
                dve.sem_inc(start, v)

            link = weights.link
            for t, v in ((w2p, 0.0), (w1p, 0.0), (b2c, 0.0), (ones16, 1.0), (ones3, 1.0), (segmul, 1.0), (tot, 0.0),
                         (seen, 0.0), (bias_last, 0.0), (zero, 0.0), (rec, 0.0), (ctxT, 0.0), (ej, 0), (fbias, 0.0),
                         (em, 0.0), (hbuf, 0.0)):
                link(nc.vector.memset(t[tuple(slice(None) for _ in t.shape)], v))
            link(nc.vector.memset(segmul[:, :, 0:1], 0.0))
            dve.wait_ge(s_w, 16 * N_LOADS)
            dve.wait_ge(s_cst, 1)
            w2v = w2f.rearrange("p (c k) -> p k c", k=TAPS)
            link(nc.vector.memset(w3p[C:P, KT - 1, :], 0.0))
            for kt, (ka, kb) in enumerate(PAIRS):
                link(nc.vector.tensor_copy(w1p[0:C, kt, :], w1f[0:C, ka, :]))
                link(nc.vector.tensor_copy(w2p[:, kt, 0:C], w2v[:, ka, :]))
                link(nc.vector.tensor_scalar(b2c[0:C, kt:kt + 1], b2f[0:C, ka:ka + 1], 0.5, None, ALU.mult))
                if kb is not None:
                    link(nc.vector.tensor_copy(w1p[C:P, kt, :], w1f[C:P, kb, :]))
                    link(nc.vector.tensor_copy(w2p[:, kt, C:P], w2v[:, kb, :]))
                    link(nc.vector.tensor_scalar(b2c[C:P, kt:kt + 1], b2f[C:P, kb:kb + 1], 0.5, None, ALU.mult))
            link(nc.vector.tensor_scalar(w3p[:, :, :], w3p[:, :, :], 0.5, None, ALU.mult))
            link(nc.vector.tensor_copy(bias_first[:, :], b3r[:, :]))
            link(nc.vector.tensor_copy(bias_first[0:1, :], clsr))
            link(nc.vector.tensor_copy(bias_last[0:TAIL, :], b3r[0:TAIL, :]))
            src = fw1f
            for w in range(WP):
                link(nc.vector.tensor_copy(fw1[:, w, :], src))
                if w + 1 < WP:
                    link(nc.vector.tensor_tensor(fw1r, src, fw1[:, w, :], ALU.subtract))
                    src = fw1r
            for w in range(WP):
                link(nc.vector.tensor_copy(fb2b, fb2f))
                link(nc.vector.tensor_scalar(fb2s, fb2b, ident[0:WP, w:w + 1], None, ALU.mult))
                if w == 0:
                    link(nc.vector.tensor_copy(fb2p[:, :], fb2s))
                else:
                    link(nc.vector.tensor_tensor(fb2p[:, :], fb2p[:, :], fb2s, ALU.add))
                if w + 1 < WP:
                    link(nc.vector.tensor_tensor(fb2f, fb2f, fb2b, ALU.subtract))
            link(nc.vector.memset(gw[:, :], 0.0))
            for a in range(2):
                link(nc.vector.tensor_copy(gw[D * a:D * a + D, E * a:E * a + E], gwf[D * a:D * a + D, :]))
            link(nc.vector.memset(sums[:, 0:1], 0.0))
            link(nc.vector.memset(sums[:, N:NP], 0.0))
            nc.vector.tensor_copy(st[:, 0, 0:1], b3r[:, 0:1]).then_inc(s_wp, 1)
            dve.wait_ge(s_wp, 1)

            def center(link, src, dst, s):
                mean = st[:, 0, s]
                link(nc.vector.tensor_reduce(mean, src, AX_X, ALU.add))
                link(nc.vector.tensor_scalar(mean, mean, 1.0 / D, None, ALU.mult))
                return nc.vector.tensor_tensor(dst, src, over(mean, D), ALU.subtract)

            def variance(link, squares, s):
                var, half, y = st[:, 1, s], st[:, 2, s], st[:, 3, s]
                link(nc.vector.tensor_reduce(var, squares, AX_X, ALU.add))
                link(nc.vector.tensor_scalar(var, var, 1.0 / D, LN_EPS, ALU.mult, ALU.add))
                link(nc.vector.tensor_scalar(half.bitcast(I32), var.bitcast(I32), 1, None,
                                             ALU.logical_shift_right))
                link(nc.vector.tensor_scalar(y.bitcast(I32), half.bitcast(I32), -1.0, float(RSQRT_MAGIC),
                                             ALU.mult, ALU.add))

            def newton(link, s, step):
                var, t = st[:, 1, s], st[:, 4, s]
                y, y2 = (st[:, 3, s], st[:, 5, s]) if step % 2 == 0 else (st[:, 5, s], st[:, 3, s])
                link(nc.vector.scalar_tensor_tensor(out=t, in0=y, scalar=-0.5, in1=y,
                                                    op0=ALU.mult, op1=ALU.mult))
                link(nc.vector.tensor_tensor(t, t, var, ALU.mult))
                link(nc.vector.scalar_tensor_tensor(out=y2, in0=t, scalar=1.5, in1=y,
                                                    op0=ALU.add, op1=ALU.mult))

            def scale(centered, out, s):
                return nc.vector.tensor_tensor(out, centered, over(st[:, 5 if NEWTON % 2 else 3, s], D), ALU.mult)

            def normalize(link, centered, squares, s):
                variance(link, squares, s)
                for step in range(NEWTON):
                    newton(link, s, step)
                return scale(centered, squares, s)

            def products(t, c, then=lambda n: None):
                if c >= 2:
                    dve.wait_ge(s_tk, t * NCH + (c - 1))
                for kt, (which, r, q) in enumerate(WINDOW):
                    n = c * KT + kt
                    dve.wait_ge(s_th, t * (NCH * KT) + (n + 1))
                    nc.vector.scalar_tensor_tensor(
                        out=prod[:, c % 2, kt, :].rearrange("p (h w) -> p h w", w=W),
                        in0=th[:, n % TH, :].rearrange("p (h w) -> p h w", w=W), scalar=1.0,
                        in1=(xpa, xpb)[which][:, r + CROWS * c:r + CROWS * (c + 1), q:q + W],
                        op0=ALU.add, op1=ALU.mult).then_inc(s_prod, 1)
                    then(n)

            def add_bias(t, j):
                dve.wait_ge(s_w3, t * NG + (j + 1))
                src = bank(TOKEN_BANK[j % 2]).rearrange("p (t d) -> p t d", d=D)
                t0, t1 = group(j)[0], group(j)[-1] + 1
                cuts = sorted({t0, t1} | ({1} if t0 == 0 else set()) | ({NT - 1} if t1 == NT else set()))
                for a, z in zip(cuts, cuts[1:]):
                    bias = bias_first if a == 0 else bias_last if a == NT - 1 else b3r
                    last = nc.vector.tensor_tensor(hbuf[:, a:z, :], src[:, a - t0:z - t0, :],
                                                   bias[:, :].unsqueeze(1).broadcast_to([P, z - a, D]), ALU.add)
                last.then_inc(s_hev, 1)
                dve.wait_ge(s_hev, t * NG + (j + 1))

            def norm_step(t, part, step, link):
                s = NORM[part]
                if step == 0:
                    link(center(link, hbuf[:, s, :], ncen[part], s))
                if step == 1:
                    link(nc.vector.tensor_tensor(nsqr[part], ncen[part], ncen[part], ALU.mult))
                    variance(link, nsqr[part], s)
                if step == 2:
                    newton(link, s, 0)
                    newton(link, s, 1)
                if step == 3:
                    newton(link, s, 2)
                    scale(ncen[part], nsqr[part], s).then_inc(s_xn, 1)

            def low_parts(t, part):
                s = NORM[part]
                dve.wait_ge(s_vh, t * NPART + (part + 1))
                dve.wait_ge(s_xn, t * NPART + (part + 1))
                nc.vector.tensor_tensor(v3[:, s, D:2 * D], nsqr[part], v3[:, s, 0:D], ALU.subtract).then_inc(s_v3, 1)

            def residual(b):
                link = postc.link
                total, inv = st[:, 6, :], st[:, 7, :]
                link(nc.vector.tensor_reduce(total, rs[:, :, :], AX_X, ALU.add))
                link(nc.vector.tensor_scalar(total, total, float(-QPAD), None, ALU.add))
                link(nc.vector.reciprocal(inv, total))
                for j in range(NG):
                    dve.wait_ge(s_fold, b * NG + (j + 1))
                    s, k = span(j), len(group(j))
                    nc.vector.tensor_tensor(
                        cen[:, s, :], bank(FOLD_BANK[j], D * k).rearrange("p (t d) -> p t d", d=D),
                        over(inv[:, s], D), ALU.mult).then_inc(s_fev, 1)
                dve.wait_ge(s_free, FROM + b)
                dve.wait_ge(s_base, FROM + b * 32)
                dve.wait_ge(s_fev, (b + 1) * NG)
                nc.vector.tensor_tensor(rec[:, :, D:2 * D], hbuf[:, :, :], cen, ALU.add).then_inc(s_h2, 1)
                dve.wait_ge(s_h2, b + 1)

            def second_center(b):
                center(postc.link, rec[:, :, D:2 * D], cen, slice(0, NT)).then_inc(s_cen, 1)

            def second_norm(b):
                dve.wait_ge(s_sq, b + 1)
                normalize(postc.link, cen, sqr, slice(0, NT)).then_inc(s_xn2, 1)

            def choose(b):
                link = postc.link
                mx, best = st[:, 8, :], st[:, 9, :]
                dve.wait_ge(s_lg, FROM + b + 1)
                link(nc.vector.tensor_tensor(lg[:, :, :], bank(LOGIT_BANK, NT * E).rearrange("p (t e) -> p t e", e=E),
                                             gbr[:, :].unsqueeze(1).broadcast_to([P, NT, E]), ALU.add))
                link(nc.vector.tensor_reduce(mx, lg[:, :, :], AX_X, ALU.max))
                nc.vector.tensor_tensor(lg[:, :, :], lg[:, :, :], over(mx, E), ALU.subtract).then_inc(s_lmx, 1)
                dve.wait_ge(s_lmx, b + 1)
                link(nc.vector.tensor_scalar(hot[:, :, :], lg[:, :, :], 0.0, float(-E), ALU.is_equal, ALU.mult))
                link(nc.vector.tensor_tensor(hot[:, :, :], eidx[:, 0:NT, :], hot[:, :, :], ALU.add))
                link(nc.vector.tensor_reduce(best, hot[:, :, :], AX_X, ALU.min))
                link(nc.vector.tensor_scalar(best, best, float(E), None, ALU.add))
                link(nc.vector.tensor_tensor(hot[:, :, :], eidx[:, 0:NT, :], over(best, E), ALU.is_equal))
                link(nc.vector.tensor_tensor(hot[:, :, :], hot[:, :, :], over(valid[:, :], E), ALU.mult))
                nc.vector.tensor_copy(hot16[:, :, :], hot[:, :, :]).then_inc(s_hot, 1)

            n, tiles, ends, first, ones = (em[:, k, :] for k in range(5))

            def place_record(b):
                link = postc.link
                esum = st[:, 10, :]
                dve.wait_ge(s_lex, b + 1)
                link(nc.vector.tensor_reduce(esum, lex[:, :, :], AX_X, ALU.add))
                link(nc.vector.reciprocal(rec[:, :, COL_P], esum))
                link(nc.vector.tensor_copy(rec[:, :, COL_ID], idf[:, :]))
                link(nc.vector.tensor_scalar(idf[:, :], idf[:, :], float(N), None, ALU.add))

            def place_counts(b):
                link = postc.link
                dve.wait_ge(s_cum, b + 1)
                link(nc.vector.tensor_copy(tot[:, :, 1:NT + 1],
                                           bank(COUNT_BANK)[:, 256:256 + NT * E].rearrange("p (t e) -> p e t", e=E)))
                link(nc.vector.tensor_tensor_scan(pre[:, :, :].rearrange("p e t -> p (e t)"),
                                                  segmul[:, :, :].rearrange("p e t -> p (e t)"),
                                                  tot[:, :, :].rearrange("p e t -> p (e t)"), 0.0,
                                                  ALU.mult, ALU.add))
                link(nc.vector.tensor_tensor(cnt[:, :, :],
                                             bank(COUNT_BANK)[:, 0:NT * E].rearrange("p (t e) -> p t e", e=E),
                                             pre[:, :, 0:NT].rearrange("p e t -> p t e"), ALU.add))
            def place_tiles(b):
                link = postc.link
                link(nc.vector.tensor_copy(n, pre[:, :, NT]))
                link(nc.vector.tensor_scalar(tiles, n, 1.0 / P, (P - 1) / P - 0.5 + 0.5 / P, ALU.mult, ALU.add))
                link(nc.vector.tensor_copy(emi[:, :], tiles))
                link(nc.vector.tensor_copy(tiles, emi[:, :]))
                link(nc.vector.memset(ones, 1.0))
                link(nc.vector.tensor_tensor_scan(ends, ones, tiles, 0.0, ALU.mult, ALU.add))
                link(nc.vector.tensor_tensor(first, ends, tiles, ALU.subtract))
                link(nc.vector.tensor_scalar(first, first, float(P), -1.0, ALU.mult, ALU.add))
            def place_slots(b):
                link = postc.link
                link(nc.vector.tensor_tensor(pen[:, :, :], cnt[:, :, :],
                                             seen[:, :].unsqueeze(1).broadcast_to([P, NT, E]), ALU.add))
                link(nc.vector.tensor_scalar(pen[:, :, :], pen[:, :, :], float(CAP), float(PAST_END),
                                             ALU.is_gt, ALU.mult))
                link(nc.vector.tensor_tensor(cnt[:, :, :], cnt[:, :, :],
                                             first.unsqueeze(1).broadcast_to([P, NT, E]), ALU.add))
                link(nc.vector.tensor_tensor(cnt[:, :, :], cnt[:, :, :], pen[:, :, :], ALU.add))
                link(nc.vector.tensor_tensor(cnt[:, :, :], cnt[:, :, :], hot[:, :, :], ALU.mult))
                link(nc.vector.tensor_reduce(slotf[:, :], cnt[:, :, :], AX_X, ALU.add))
                link(nc.vector.tensor_tensor(slotf[:, :], slotf[:, :], pastend[:, :], ALU.add))
                nc.vector.tensor_copy(slot[:, :], slotf[:, :]).then_inc(s_slot, 1)
                link(nc.vector.tensor_tensor(seen[:, :], seen[:, :], n, ALU.add))
            def place_experts(b):
                link = postc.link
                link(nc.vector.tensor_tensor(ehot[:, :, :], tileno[:, :, :],
                                             ends.unsqueeze(1).broadcast_to([P, FT, E]), ALU.is_ge))
                link(nc.vector.tensor_reduce(ejf[:, :], ehot[:, :, :], AX_X, ALU.add))
                link(nc.vector.tensor_scalar(ejf[:, :], ejf[:, :], float(E - 1), None, ALU.min))
                link(nc.vector.tensor_tensor(ehot[:, :, :], eidx[:, :, :], over(ejf[:, :], E), ALU.is_equal))
                link(nc.vector.tensor_copy(fbias[:, :, 0:HT], fbias[:, :, FT:LT]))
                link(nc.vector.tensor_copy(ej[:, 0:HT], ej[:, FT:LT]))
                for f in range(NF):
                    link(nc.vector.tensor_tensor(eprod[:, :, :], ehot[:, :, :],
                                                 fb1c[:, :, f].unsqueeze(1).broadcast_to([P, FT, E]), ALU.mult))
                    link(nc.vector.tensor_reduce(fbias[:, f, HT:LT], eprod[:, :, :], AX_X, ALU.add))
                nc.vector.tensor_copy(ej[:, HT:LT], ejf[:, :]).then_inc(s_ej, 1)
                dve.wait_ge(s_ej, FROM + b + 1)

            def mix(b, post, tok):
                t = b + 1
                tokc.at(t)
                postc.at(b)
                pieces = {4: (residual,), 5: (second_center,), 9: (second_norm,), 17: (choose,), 20: (place_record,),
                          21: (place_counts,), 22: (place_tiles,), 23: (place_slots,), 24: (place_experts,)}

                def then(n):
                    for piece in pieces.get(n, ()) if post else ():
                        piece(b)
                    if n == 27 and post:
                        dve.wait_ge(s_rl, b + 1)
                    if 27 <= n < 31:
                        norm_step(t, 0, n - 27, tokc.link)

                if tok:
                    for c in range(NCH):
                        products(t, c, then)
                        if c == 4:
                            add_bias(t, 0)
                    low_parts(t, 0)
                    tokc.ends()
                else:
                    for some in pieces.values():
                        for piece in some:
                            piece(b)
                if post:
                    postc.ends()

            def attention(b):
                base = b * STEPS
                normc.at(b)
                expc.at(b * 2)
                add_bias(b, 1)
                for step in range(4):
                    norm_step(b, 1, step, normc.link)
                add_bias(b, 2)
                add_bias(b, 3)
                low_parts(b, 1)
                for g in range(STEPS):
                    dve.wait_ge(s_exp, base + (g + 1))
                    dve.wait_ge(s_pv, FROM + base + max(g - HR + 1, 0))
                    if not twice(g):
                        nc.vector.tensor_copy(eh[:, g % HR, :], e32[:, g % ER, :]).then_inc(s_eh, 1)
                        dve.wait_ge(s_eh, b * CASTS + casts(g + 1))
                    nc.vector.tensor_tensor(el[:, g % HR, :], e32[:, g % ER, :], eh[:, g % HR, :],
                                            ALU.subtract).then_inc(s_el, 1)
                    for step in range(4):
                        if g == NORM_STEPS[step]:
                            norm_step(b, 2, step, normc.link)
                    if g == LOW_STEP:
                        low_parts(b, 2)
                    for q in range(4):
                        if g in FINISH_STEPS[q]:
                            finish_group(b, q // 2, q % 2, FINISH_STEPS[q].index(g))
                normc.ends()

            def finish_group(i, p, r, part):
                link = expc.link
                fz3 = fz[:, r, :].rearrange("p (g d) -> p g d", d=D)
                fo3 = fo[:, r, :].rearrange("p (g d) -> p g d", d=D)
                if part == 0:
                    dve.wait_ge(f_ye, FROM + i * 4 + (p * 2 + (r + 1)))
                    link(nc.vector.tensor_scalar(fstale[:, r, :], frec[:, r, :, COL_ID], oldest[:, bass.ds(p, 1)],
                                                 float(PAST_END), ALU.is_lt, ALU.mult))
                if part == 1:
                    dve.wait_ge(f_free, i * 4 + p * 2 + (r + 1))
                    link(nc.vector.tensor_tensor(fidx[:, r, :], fstale[:, r, :], frec[:, r, :, COL_ID], ALU.add))
                if part == 2:
                    link(nc.vector.tensor_tensor(fz3, fz3, frec[:, r, :, COL_P:COL_P + 1].broadcast_to([P, GT, D]),
                                                 ALU.mult))
                if part == 3:
                    link(nc.vector.tensor_scalar(fmask, fz[:, r, :], 0.0, 0.0, ALU.mult, ALU.is_equal))
                if part == 4:
                    link(nc.vector.tensor_tensor(fnan, fz[:, r, :], fz[:, r, :], ALU.not_equal))
                if part == 5:
                    link(nc.vector.tensor_scalar(fo[:, r, :], fz[:, r, :], -1e4, 1e4, ALU.max, ALU.min), apart=True)
                if part == 6:
                    link(nc.vector.copy_predicated(fo[:, r, :], fmask, fz[:, r, :]), apart=True)
                if part == 7:
                    link(nc.vector.copy_predicated(fo[:, r, :], fnan, zero[:, :]))
                if part == 8:
                    nc.vector.tensor_tensor(fo3, fo3, frec[:, r, :, D:2 * D], ALU.add).then_inc(f_o, 1)

            def last_experts(p):
                expc.at(B * 2 + p)
                for r in range(2):
                    for part in range(FINISH):
                        finish_group(B, p, r, part)
                expc.ends()

            def next_oldest(i):
                dve.wait_ge(f_o, FROM2 + i * 4 + 4)
                nc.vector.tensor_scalar(oldest[:, :], oldest[:, :], float(N), None, ALU.add).then_inc(s_old, 1)
                dve.wait_ge(s_old, i + 1)

            def attend(b):
                attention(b)
                next_oldest(b)

            mix(-1, False, True)
            with dve.Fori(0, B - 1) as b:
                attend(b)
                mix(b, True, True)
            attend(B - 1)
            mix(B - 1, True, False)
            with dve.Fori(0, 3) as p:
                last_experts(p)


_INS = ['x', 'cls_tok', 'L0_tok_W1', 'L0_tok_b1', 'L0_tok_W2', 'L0_tok_b2', 'L0_tok_W3', 'L0_tok_b3',
        'L0_ffn_gate_w', 'L0_ffn_gate_b', 'L0_ffn_w1', 'L0_ffn_b1', 'L0_ffn_w2', 'L0_ffn_b2']


def kernel(**inputs):
    import numpy as _np
    import concourse.bacc as _bacc
    from concourse import mybir as _mybir
    from concourse.bass_utils import run_bass_kernel_spmd as _run

    nc = _bacc.Bacc("TRN2", target_bir_lowering=False, num_devices=1)
    arrays, args = {}, []
    for name in _INS:
        a = _np.ascontiguousarray(inputs[name])
        arrays[f"in_{name}_dram"] = a
        args.append(nc.dram_tensor(f"in_{name}_dram", a.shape, _mybir.dt.from_np(a.dtype), kind="ExternalInput").ap())
    B, C, H, W = inputs["x"].shape
    args.append(nc.dram_tensor("out_0_dram", (B, H * W + 1, C), _mybir.dt.float32, kind="ExternalOutput").ap())
    vit_block_kernel(nc, *args)
    r = _run(nc, [arrays], core_ids=[0])
    return r.results[0]["out_0_dram"]
```
